# Optimizing a Trainium2 kernel written in Bass

```python
import numpy as np
import jax
import jax.numpy as jnp

def _softmax(x, axis=-1):
    return jax.nn.softmax(x, axis=axis)

def _gelu(x):
    return jax.nn.gelu(x, approximate=True)

def _silu(x):
    return jax.nn.silu(x)

def _sigmoid(x):
    return jax.nn.sigmoid(x)

def _layernorm(x, axis=-1, eps=1e-05):
    m = jnp.mean(x, axis=axis, keepdims=True)
    v = jnp.var(x, axis=axis, keepdims=True)
    return (x - m) / jnp.sqrt(v + eps)

def _scatter_add(tgt, idx, src, axis=0):
    return tgt.at[idx].add(src)

def _segment_sum(src, seg, n):
    return jax.ops.segment_sum(src, seg, n)
kernel_name = 'mk_cond_resid_d2_seqx_r4_539967'

def setup_inputs(seed: int=0):
    np.random.seed(seed)
    _w = jnp.asarray

    def _rec_inputs():
        import jax
        import jax.numpy as jnp
        _rk = jax.random.key(seed)
        x = -0.000125 + 0.9999 * jax.random.normal(jax.random.fold_in(_rk, 1), (64, 64, 256), jnp.float32)
        _lenS = 64 - jax.random.randint(jax.random.fold_in(_rk, 7), (64,), 0, max(1, 64 // 4) + 1, jnp.int32)
        _lenS2 = 64 - jax.random.randint(jax.random.fold_in(_rk, 8), (64,), 0, max(1, 64 // 4) + 1, jnp.int32)
        cond_512 = 0.0061147 + 1.02565 * jax.random.normal(jax.random.fold_in(_rk, 11), (64, 128), jnp.float32)
        return (x, cond_512)
    x, cond_512 = _rec_inputs()

    def _L0_cond_setup():
        import jax, jax.numpy as jnp
        import numpy as np
        B, S, D, H, C = (8, 1024, 256, 64, 128)
        INIT_RANGE = 0.01
        key = jax.random.key(seed)
        ks = jax.random.split(key, 6)
        return {'hidden_states': jax.random.normal(ks[0], (B, S, D), dtype=jnp.float32), 'conditions': jax.random.normal(ks[1], (B, C), dtype=jnp.float32), 'down_project': jax.random.normal(ks[2], (D, H), dtype=jnp.float32) * INIT_RANGE, 'down_gamma': jax.random.normal(ks[3], (C, H), dtype=jnp.float32), 'down_beta': jnp.zeros((C, H), dtype=jnp.float32), 'up_project': jax.random.normal(ks[4], (H, D), dtype=jnp.float32) * INIT_RANGE, 'up_gamma': jax.random.normal(ks[5], (C, D), dtype=jnp.float32), 'up_beta': jnp.zeros((C, D), dtype=jnp.float32)}
    _L0_cond_all = _L0_cond_setup()
    _L0_cond_in = {k: v for k, v in _L0_cond_all.items() if k in ('down_project', 'down_gamma', 'down_beta', 'up_project', 'up_gamma', 'up_beta')}
    del _L0_cond_all

    def _L1_cond_setup():
        import jax, jax.numpy as jnp
        import numpy as np
        W_DIM = 128
        CLAMP = 256.0
        key = jax.random.key(seed)
        ks = jax.random.split(key, 6)
        B, L, C = (8, 2048, 256)
        return {'x': jax.random.normal(ks[0], (B, L, C), dtype=jnp.float32), 'w': jax.random.normal(ks[1], (B, W_DIM), dtype=jnp.float32), 'weight': jax.random.normal(ks[2], (C, C), dtype=jnp.float32), 'bias': jax.random.normal(ks[3], (C,), dtype=jnp.float32), 'affine_w': jax.random.normal(ks[4], (C, W_DIM), dtype=jnp.float32), 'affine_b': jnp.ones((C,), dtype=jnp.float32)}
    _L1_cond_all = _L1_cond_setup()
    _L1_cond_in = {k: v for k, v in _L1_cond_all.items() if k in ('weight', 'bias', 'affine_w', 'affine_b')}
    del _L1_cond_all
    return {'x': x, 'cond_512': cond_512, 'L0_cond_down_project': _L0_cond_in['down_project'], 'L0_cond_down_gamma': _L0_cond_in['down_gamma'], 'L0_cond_down_beta': _L0_cond_in['down_beta'], 'L0_cond_up_project': _L0_cond_in['up_project'], 'L0_cond_up_gamma': _L0_cond_in['up_gamma'], 'L0_cond_up_beta': _L0_cond_in['up_beta'], 'L1_cond_weight': _L1_cond_in['weight'], 'L1_cond_bias': _L1_cond_in['bias'], 'L1_cond_affine_w': _L1_cond_in['affine_w'], 'L1_cond_affine_b': _L1_cond_in['affine_b']}

def reference(x, cond_512, L0_cond_down_project, L0_cond_down_gamma, L0_cond_down_beta, L0_cond_up_project, L0_cond_up_gamma, L0_cond_up_beta, L1_cond_weight, L1_cond_bias, L1_cond_affine_w, L1_cond_affine_b):
    import jax
    import jax.numpy as jnp

    def _L0_cond_ref(hidden_states, conditions, down_project, down_gamma, down_beta, up_project, up_gamma, up_beta):
        import jax, jax.numpy as jnp
        import numpy as np
        B, S, D, H, C = (8, 1024, 256, 64, 128)
        INIT_RANGE = 0.01
        dg = conditions @ down_gamma
        db = conditions @ down_beta
        ug = conditions @ up_gamma
        ub = conditions @ up_beta
        w_down = down_project[None, :, :] * dg[:, None, :] + db[:, None, :]
        down = jnp.einsum('bsd,bdh->bsh', hidden_states, w_down)
        act = jax.nn.relu(down)
        w_up = up_project[None, :, :] * ug[:, None, :] + ub[:, None, :]
        up = jnp.einsum('bsh,bhd->bsd', act, w_up)
        return up + hidden_states

    def _L1_cond_ref(x, w, weight, bias, affine_w, affine_b):
        import jax, jax.numpy as jnp
        import numpy as np
        W_DIM = 128
        CLAMP = 256.0
        B, L, C = x.shape
        gain = 1.0 / np.sqrt(W_DIM).astype(np.float32)
        styles = w @ (affine_w * gain).T + affine_b
        ws = weight[None, :, :] * styles[:, None, :]
        dcoefs = jax.lax.rsqrt(jnp.sum(ws * ws, axis=2) + 1e-08)
        xm = x * styles[:, None, :]
        y = jnp.einsum('blc,oc->blo', xm, weight)
        y = y * dcoefs[:, None, :]
        y = jnp.clip(y + bias, -CLAMP, CLAMP)
        return y
    x = x + _L0_cond_ref(x, cond_512, L0_cond_down_project, L0_cond_down_gamma, L0_cond_down_beta, L0_cond_up_project, L0_cond_up_gamma, L0_cond_up_beta)
    x = x + _L1_cond_ref(x, cond_512, L1_cond_weight, L1_cond_bias, L1_cond_affine_w, L1_cond_affine_b)
    return x

_drawn_inputs = setup_inputs


def setup_inputs(seed=0):
    import zlib

    import numpy as np

    out = dict(_drawn_inputs(seed))
    spreads = {'L0_cond_down_beta': (0.0, 0.1),
     'L0_cond_up_beta': (0.0, 0.1),
     'L1_cond_affine_b': (1.0, 0.2)}
    factors = {'L1_cond_bias': 49.459}
    for name, (base, spread) in spreads.items():
        noise = np.random.default_rng([zlib.crc32(name.encode()), seed]).standard_normal(out[name].shape)
        drawn = base * np.exp(spread * noise) if base else spread * noise
        out[name] = jnp.asarray(drawn.astype(out[name].dtype))
    for name, factor in factors.items():
        out[name] = (out[name] * factor).astype(out[name].dtype)
    return out
```

```python
from collections import namedtuple
from contextlib import ExitStack

import concourse.bass as bass
from concourse import mybir

ALU = mybir.AluOpType
ACT = mybir.ActivationFunctionType
F32 = mybir.dt.float32
F32R = mybir.dt.float32r

P = 128
Tile = namedtuple("Tile", "n parity half")
CLAMP = 256.0
EPS = 1e-8


def bass_cond_resid(nc, x, cond, down_project, down_gamma, down_beta, up_project, up_gamma, up_beta,
                    weight, bias, affine_w, affine_b, out):
    B, S, D = x.shape
    H = down_project.shape[1]
    C = cond.shape[1]
    DC = D // P
    T = 512
    TB = T // S
    TILES = B * S // T
    TJ = T // P
    HT = T // 2
    HB = TB // 2
    GAIN = float(C) ** -0.5
    assert H == P // 2 and C == P and DC == 2 and TILES >= 8 and TILES % 2 == 0

    x_tiles = x.rearrange("b s d -> (b s) d").rearrange("(t j p) d -> t p j d", p=P, j=TJ)
    out_tiles = out.rearrange("b s d -> (b s) d").rearrange("(t j p) d -> t p j d", p=P, j=TJ)

    with ExitStack() as ctx:
        def sb(name, shape, dt=F32):
            return ctx.enter_context(nc.sbuf_tensor(name, shape, dt))

        def psum(name, shape):
            return ctx.enter_context(nc.psum_tensor(name, shape, F32))

        def sem(name):
            return ctx.enter_context(nc.semaphore(name))

        ident = sb("ident", [P, P])
        ones = sb("ones", [P, H])
        ones_r = sb("ones_r", [P, P], F32R)
        cond_sb = sb("cond_sb", [B, C])
        condT = sb("condT", [C, B])
        dp_sb = sb("dp_sb", [P, DC, H])
        dgb_sb = sb("dgb_sb", [C, 2, H])
        up_sb = sb("up_sb", [P, D])
        up_hi = sb("up_hi", [P, D], F32R)
        up_lo = sb("up_lo", [P, D], F32R)
        ugb_sb = sb("ugb_sb", [C, 2, D])
        w_sb = sb("w_sb", [P, DC, D])
        wT = sb("wT", [P, DC, D])
        wT_sq = sb("wT_sq", [P, DC, D])
        aff_sb = sb("aff_sb", [P, DC, C])
        affT = sb("affT", [C, D])
        vec_rows = sb("vec_rows", [2 * DC, P])
        vec_cols = sb("vec_cols", [P, 2 * DC])
        down_tab = sb("down_tab", [P, 2, TILES, HB])
        up_tab = sb("up_tab", [P, 2, DC, B])
        style = sb("style", [P, DC, B])
        style_sq = sb("style_sq", [P, DC, B])
        demod = sb("demod", [P, DC, B])
        dm_q = sb("dm_q", [P, DC, B])
        dm_r = sb("dm_r", [P, DC, B])
        dm_t = sb("dm_t", [P, DC, B])

        x_nat = sb("x_nat", [P, 2, TJ, D])
        xT = sb("xT", [P, 2, DC, T])
        down_sc = sb("down_sc", [P, 2, HT])
        pre = sb("pre", [P, HT])
        act_hl = sb("act_hl", [P, 2, T], F32R)
        up_sc = sb("up_sc", [P, DC, T])
        off_sc = sb("off_sc", [P, DC, T])
        up_sum = sb("up_sum", [P, DC, T])
        x2 = sb("x2", [P, TILES, DC, T])
        xm = sb("xm", [P, 2, DC, T])
        y_sc = sb("y_sc", [P, DC, T])
        y_cl = sb("y_cl", [P, DC, T])
        z = sb("z", [P, 2, DC, T])
        out_nat = sb("out_nat", [P, TILES, TJ, D])

        ps_io = psum("ps_io", [P, 2 * T])
        ps_down = psum("ps_down", [P, 2, HT])
        ps_sum = psum("ps_sum", [P, T])
        ps_up = psum("ps_up", [P, DC, T])
        ps_y = psum("ps_y", [P, DC, T])

        x_loaded = [sem(f"x_loaded{i}") for i in range(2)]
        out_stored = sem("out_stored")
        cond_in, dp_in, dgb_in, up_in = sem("cond_in"), sem("dp_in"), sem("dgb_in"), sem("up_in")
        ugb_in, w_in, aff_in, vec_in = sem("ugb_in"), sem("w_in"), sem("aff_in"), sem("vec_in")
        zeroed, ident_ready, ones_ready = sem("zeroed"), sem("ident_ready"), sem("ones_ready")
        condT_ps, condT_sb = sem("condT_ps"), sem("condT_sb")
        dtab_ps, dtab_sb = sem("dtab_ps"), sem("dtab_sb")
        utab_ps, utab_sb = sem("utab_ps"), sem("utab_sb")
        affT_ps, affT_sb = sem("affT_ps"), sem("affT_sb")
        wT_ps, wT_sb, wsq_ready = sem("wT_ps"), sem("wT_sb"), sem("wsq_ready")
        style_ps, style_sb, ssq_ready = sem("style_ps"), sem("style_sb"), sem("ssq_ready")
        norm_ps, norm_sb, root_done, newton = sem("norm_ps"), sem("norm_sb"), sem("root_done"), sem("newton")
        up_hi_ready, up_lo_ready = sem("up_hi_ready"), sem("up_lo_ready")

        xT_ps, xT_sb, x_doubled = sem("xT_ps"), sem("xT_sb"), sem("x_doubled")
        down_ps, down_scaled, pre_ready = sem("down_ps"), sem("down_scaled"), sem("pre_ready")
        hi_ready, lo_ready = sem("hi_ready"), sem("lo_ready")
        up_ps, up_scaled, off_scaled, up_summed = sem("up_ps"), sem("up_scaled"), sem("off_scaled"), sem("up_summed")
        x2_ready, xm_ready = sem("x2_ready"), sem("xm_ready")
        y_ps = [sem(f"y_ps{c}") for c in range(DC)]
        y_scaled = [sem(f"y_scaled{c}") for c in range(DC)]
        y_capped = [sem(f"y_capped{c}") for c in range(DC)]
        z_ready = [sem(f"z_ready{c}") for c in range(DC)]
        z_ps, out_ready = sem("z_ps"), sem("out_ready")

        FIRST = 3
        PAIRS = (TILES - 1 - FIRST) // 2

        def steps(eng, step):
            def peeled(k):
                def tile(lag):
                    n = k - lag
                    return Tile(n, n % 2, n // 2) if 0 <= n < TILES else None
                step(tile, k)

            for k in range(FIRST):
                peeled(k)
            with eng.Fori(0, PAIRS) as pair:
                for u in range(2):
                    def tile(lag):
                        k = FIRST + u - lag
                        return Tile(2 * pair + k, k % 2, pair + k // 2)
                    step(tile, None)
            for k in range(FIRST + 2 * PAIRS, TILES + 3):
                peeled(k)

        def wait(eng, s, count):
            if not isinstance(count, int) or count > 0:
                eng.wait_ge(s, count)

        def per_batch(table):
            return table.unsqueeze(3).to_broadcast([P, table.shape[1], table.shape[2], S])

        def by_batch(tile):
            return tile.rearrange("p c (b s) -> p c b s", s=S)

        block = ctx.enter_context(nc.Block())

        @block.sync
        def _(sp):
            def load(n, parity):
                wait(sp, xT_ps, n - 1)
                sp.dma_start(x_nat[:, parity], x_tiles[n]).then_inc(x_loaded[parity], 16)

            sp.dma_start(cond_sb[:], cond).then_inc(cond_in, 16)
            load(0, 0)
            sp.dma_start(dp_sb[:], down_project.rearrange("(c p) h -> p c h", p=P)).then_inc(dp_in, 16)
            sp.dma_start(aff_sb[:], affine_w.rearrange("(c p) w -> p c w", p=P)).then_inc(aff_in, 16)
            load(1, 1)
            sp.dma_start(w_sb[:], weight.rearrange("(o p) c -> p o c", p=P)).then_inc(w_in, 16)
            with sp.Fori(1, TILES // 2) as pair:
                for parity in range(2):
                    load(2 * pair + parity, parity)
            with sp.Fori(0, TILES) as n:
                sp.wait_ge(out_ready, n + 2)
                sp.dma_start(out_tiles[n], out_nat[:, n]).then_inc(out_stored, 16)
            sp.wait_ge(out_stored, 16 * TILES)

        @block.scalar
        def _(act):
            act.dma_start(vec_rows[0:DC], affine_b.rearrange("(c p) -> c p", p=P)).then_inc(vec_in, 16)
            act.dma_start(vec_rows[DC:2 * DC], bias.rearrange("(c p) -> c p", p=P)).then_inc(vec_in, 16)
            act.dma_start(dgb_sb[:, 0], down_gamma).then_inc(dgb_in, 16)
            act.dma_start(dgb_sb[:, 1], down_beta).then_inc(dgb_in, 16)
            act.dma_start(up_sb[0:H, :], up_project).then_inc(up_in, 16)
            act.dma_start(up_sb[H:P, :], up_project).then_inc(up_in, 16)
            act.dma_start(ugb_sb[:, 0], up_gamma).then_inc(ugb_in, 16)
            act.dma_start(ugb_sb[:, 1], up_beta).then_inc(ugb_in, 16)

            act.wait_ge(condT_ps, 1)
            act.activation(condT[:], ps_sum[:, 0:B], ACT.Copy)
            act.activation(vec_cols[:], ps_sum[:, B:B + 2 * DC], ACT.Copy).then_inc(condT_sb, 1)

            act.sem_inc(out_ready, 1)

            def evacuate_xT(t):
                act.wait_ge(xT_ps, t.n + 1)
                wait(act, down_ps, t.n - 1)
                act.activation(xT[:, t.parity].rearrange("p c t -> p (c t)"), ps_io[:], ACT.Copy).then_inc(xT_sb, 1)
                act.activation(x2[:, t.n].rearrange("p c t -> p (c t)"), ps_io[:], ACT.Copy,
                               scale=2.0).then_inc(x_doubled, 1)

            def relu_high(t):
                act.wait_ge(pre_ready, t.n + 1)
                wait(act, up_ps, t.n - 1)
                act.activation(act_hl[0:H, t.parity, 0:HT], pre[0:H, :], ACT.Relu)
                act.activation(act_hl[H:P, t.parity, HT:T], pre[H:P, :], ACT.Relu).then_inc(hi_ready, 1)

            def evacuate_out(t):
                act.wait_ge(z_ps, t.n + 1)
                act.activation(out_nat[:, t.n].rearrange("p j d -> p (j d)"), ps_io[:], ACT.Copy).then_inc(out_ready, 1)

            evacuate_xT(Tile(0, 0, 0))
            act.wait_ge(affT_ps, 1)
            act.activation(affT[:], ps_up[:, 1, 0:D], ACT.Copy).then_inc(affT_sb, 1)
            act.wait_ge(up_in, 32)
            act.activation(up_hi[:], up_sb[:], ACT.Copy).then_inc(up_hi_ready, 1)

            def styles():
                act.wait_ge(condT_sb, 1)
                act.wait_ge(style_ps, 1)
                for c in range(DC):
                    last = act.activation(style[:, c], ps_sum[:, c * B:(c + 1) * B], ACT.Identity,
                                          bias=vec_cols[:, c:c + 1], scale=GAIN)
                last.then_inc(style_sb, 1)
                act.wait_ge(wT_ps, 1)
                act.activation(wT[:].rearrange("p c o -> p (c o)"), ps_y[:, 0], ACT.Copy).then_inc(wT_sb, 1)

            def root():
                act.wait_ge(norm_sb, 1)
                act.activation(dm_t[:], dm_q[:], ACT.Sqrt).then_inc(root_done, 1)

            def step(tile, first):
                if tile(0):
                    relu_high(tile(0))
                if tile(-1):
                    evacuate_xT(tile(-1))
                if first == 0:
                    root()
                if tile(3):
                    evacuate_out(tile(3))
            styles()
            steps(act, step)

        @block.vector
        def _(dve):
            dve.memset(ones[:], 1.0)
            dve.memset(ones_r[:].bitcast(F32), 1.0).then_inc(ones_ready, 1)

            dve.wait_ge(dtab_ps, 1)
            for g in range(2):
                for half in range(2):
                    rows = slice(half * H, (half + 1) * H)
                    src = ps_y[rows, 1, g * B:(g + 1) * B].rearrange("p (t b) -> p t b", b=TB)
                    last = dve.tensor_copy(down_tab[rows, g], src[:, :, half * HB:(half + 1) * HB])
            last.then_inc(dtab_sb, 1)

            def tables():
                dve.wait_ge(utab_ps, 1)
                dve.tensor_copy(up_tab[:].rearrange("p g c b -> p (g c b)"), ps_up[:, 0, 0:2 * DC * B]).then_inc(utab_sb, 1)
                dve.wait_ge(up_hi_ready, 1)
                dve.tensor_tensor(up_lo[:], up_sb[:], up_hi[:].bitcast(F32), ALU.subtract).then_inc(up_lo_ready, 1)

            def squares():
                dve.wait_ge(style_sb, 1)
                dve.tensor_tensor(style_sq[:], style[:], style[:], ALU.mult).then_inc(ssq_ready, 1)
                dve.wait_ge(wT_sb, 1)
                dve.tensor_tensor(wT_sq[:], wT[:], wT[:], ALU.mult).then_inc(wsq_ready, 1)
                dve.wait_ge(norm_ps, 1)
                dve.tensor_scalar(dm_q[:].rearrange("p c b -> p (c b)"), ps_y[:, 1, 0:DC * B], EPS, None,
                                  ALU.add).then_inc(norm_sb, 1)

            def demodulation():
                dve.wait_ge(root_done, 1)
                dve.reciprocal(dm_r[:], dm_t[:]).then_inc(newton, 1)
                dve.wait_ge(newton, 1)
                dve.tensor_tensor(dm_t[:], dm_r[:], dm_r[:], ALU.mult).then_inc(newton, 1)
                dve.wait_ge(newton, 2)
                dve.tensor_tensor(dm_q[:], dm_t[:], dm_q[:], ALU.mult).then_inc(newton, 1)
                dve.wait_ge(newton, 3)
                dve.tensor_scalar(dm_t[:], dm_q[:], -0.5, 1.5, ALU.mult, ALU.add).then_inc(newton, 1)
                dve.wait_ge(newton, 4)
                dve.tensor_tensor(demod[:], dm_t[:], dm_r[:], ALU.mult).then_inc(newton, 1)
                dve.wait_ge(newton, 5)

            def scale_down(t):
                dve.wait_ge(down_ps, t.n + 1)
                wait(dve, pre_ready, t.n)
                tab = down_tab[:, :, t.n, :].unsqueeze(3).to_broadcast([P, 2, HB, S])
                dve.tensor_tensor(by_batch(down_sc[:]), by_batch(ps_down[:]), tab, ALU.mult).then_inc(down_scaled, 1)

            def relu_low(t):
                dve.wait_ge(hi_ready, t.n + 1)
                dve.scalar_tensor_tensor(out=act_hl[H:P, t.parity, 0:HT], in0=pre[0:H, :], scalar=0.0,
                                         in1=act_hl[0:H, t.parity, 0:HT].bitcast(F32), op0=ALU.max, op1=ALU.subtract)
                dve.scalar_tensor_tensor(out=act_hl[0:H, t.parity, HT:T], in0=pre[H:P, :], scalar=0.0,
                                         in1=act_hl[H:P, t.parity, HT:T].bitcast(F32), op0=ALU.max,
                                         op1=ALU.subtract).then_inc(lo_ready, 1)

            def scale_up(t):
                dve.wait_ge(up_ps, t.n + 1)
                wait(dve, up_summed, t.n)
                batches = bass.ds(t.n * TB, TB)
                dve.tensor_tensor(by_batch(up_sc[:]), by_batch(ps_up[:]), per_batch(up_tab[:, 0, :, batches]),
                                  ALU.mult).then_inc(up_scaled, 1)
                sums = by_batch(ps_sum[:].unsqueeze(1).to_broadcast([P, DC, T]))
                dve.tensor_tensor(by_batch(off_sc[:]), sums, per_batch(up_tab[:, 1, :, batches]),
                                  ALU.mult).then_inc(off_scaled, 1)

            def residual(t):
                dve.wait_ge(up_summed, t.n + 1)
                dve.wait_ge(x_doubled, t.n + 1)
                dve.tensor_tensor(x2[:, t.n], x2[:, t.n], up_sum[:], ALU.add).then_inc(x2_ready, 1)

            def finish(t, c):
                dve.wait_ge(y_ps[c], t.n + 1)
                tab = demod[:, c, bass.ds(t.n * TB, TB)].unsqueeze(2).to_broadcast([P, TB, S])
                dve.tensor_tensor(y_sc[:, c].rearrange("p (b s) -> p b s", s=S),
                                  ps_y[:, c].rearrange("p (b s) -> p b s", s=S), tab, ALU.mult).then_inc(y_scaled[c], 1)
                dve.wait_ge(y_scaled[c], t.n + 1)
                dve.tensor_scalar(y_cl[:, c], y_sc[:, c], vec_cols[:, DC + c:DC + c + 1], CLAMP, ALU.add,
                                  ALU.min).then_inc(y_capped[c], 1)
                dve.wait_ge(y_capped[c], t.n + 1)
                dve.scalar_tensor_tensor(out=z[:, t.parity, c], in0=y_cl[:, c], scalar=-CLAMP, in1=x2[:, t.n, c],
                                         op0=ALU.max, op1=ALU.add).then_inc(z_ready[c], 1)

            def step(tile, first):
                if first == 0:
                    dve.wait_ge(dtab_sb, 1)
                if tile(0):
                    scale_down(tile(0))
                if first == 0:
                    tables()
                if tile(3):
                    finish(tile(3), 1)
                if tile(0):
                    relu_low(tile(0))
                if first == 0:
                    squares()
                    dve.wait_ge(utab_sb, 1)
                if tile(1):
                    scale_up(tile(1))
                if first == 1:
                    dve.wait_ge(condT_sb, 1)
                    demodulation()
                if tile(2):
                    finish(tile(2), 0)
                if tile(1):
                    residual(tile(1))
            steps(dve, step)

        @block.gpsimd
        def _(pool):
            pool.memset(ident[:], 0.0).then_inc(zeroed, 1)
            pool.wait_ge(zeroed, 1)
            pool.affine_select(out=ident[:], in_=ident[:], compare_op=ALU.not_equal, fill=1.0, base=0,
                               pattern=[[-1, P]], channel_multiplier=1).then_inc(ident_ready, 1)

            def sum_down(t):
                pool.wait_ge(down_scaled, t.n + 1)
                wait(pool, hi_ready, t.n)
                wait(pool, lo_ready, t.n)
                pool.tensor_tensor(pre[:], down_sc[:, 0], down_sc[:, 1], ALU.add).then_inc(pre_ready, 1)

            def sum_up(t):
                pool.wait_ge(up_scaled, t.n + 1)
                pool.wait_ge(off_scaled, t.n + 1)
                wait(pool, x2_ready, t.n)
                pool.tensor_tensor(up_sum[:], up_sc[:], off_sc[:], ALU.add).then_inc(up_summed, 1)

            def modulate(t):
                pool.wait_ge(x2_ready, t.n + 1)
                wait(pool, y_ps[DC - 1], t.n - 1)
                pool.tensor_tensor(by_batch(xm[:, t.parity]), by_batch(x2[:, t.n]),
                                   per_batch(style[:, :, bass.ds(t.n * TB, TB)]), ALU.mult).then_inc(xm_ready, 1)

            def step(tile, first):
                if tile(0):
                    sum_down(tile(0))
                if tile(1):
                    sum_up(tile(1))
                    if first == 1:
                        pool.wait_ge(style_sb, 1)
                    modulate(tile(1))
            steps(pool, step)

        @block.tensor
        def _(pe):
            def transpose_in(t):
                pe.wait_ge(x_loaded[t.parity], 16 * (t.half + 1))
                wait(pe, x_doubled, t.n)
                wait(pe, out_ready, t.n - 3)
                for c in range(DC):
                    for j in range(TJ):
                        last = pe.transpose(ps_io[:, c * T + j * P:c * T + (j + 1) * P],
                                            x_nat[:, t.parity, j, c * P:(c + 1) * P], ident[:])
                last.then_inc(xT_ps, 1)

            def down(t):
                pe.wait_ge(xT_sb, t.n + 1)
                wait(pe, down_scaled, t.n)
                for g in range(2):
                    for c in range(DC):
                        for half in range(2):
                            last = pe.matmul(ps_down[half * H:(half + 1) * H, g],
                                             dp_sb[:, c] if g == 0 else ones[:],
                                             xT[:, t.parity, c, half * HT:(half + 1) * HT],
                                             start=(c == 0), stop=(c == DC - 1))
                last.then_inc(down_ps, 1)

            def up(t):
                pe.wait_ge(hi_ready, t.n + 1)
                pe.wait_ge(lo_ready, t.n + 1)
                wait(pe, up_scaled, t.n)
                wait(pe, off_scaled, t.n)
                for c in range(DC):
                    pe.matmul(ps_up[:, c], up_hi[:, c * P:(c + 1) * P], act_hl[:, t.parity], start=True, stop=False)
                    pe.matmul(ps_up[:, c], up_lo[:, c * P:(c + 1) * P], act_hl[:, t.parity], start=False, stop=True)
                pe.matmul(ps_sum[:], ones_r[:], act_hl[:, t.parity], start=True, stop=True).then_inc(up_ps, 1)

            def linear(t, o):
                pe.wait_ge(xm_ready, t.n + 1)
                wait(pe, y_scaled[o], t.n)
                for c in range(DC):
                    last = pe.matmul(ps_y[:, o], wT[:, c, o * P:(o + 1) * P], xm[:, t.parity, c],
                                     start=(c == 0), stop=(c == DC - 1))
                last.then_inc(y_ps[o], 1)

            def transpose_out(t):
                for c in range(DC):
                    pe.wait_ge(z_ready[c], t.n + 1)
                pe.wait_ge(x_doubled, min(t.n + 5, TILES) if isinstance(t.n, int) else t.n + 5)
                pe.wait_ge(out_ready, t.n + 1)
                for j in range(TJ):
                    for c in range(DC):
                        last = pe.transpose(ps_io[:, j * D + c * P:j * D + (c + 1) * P],
                                            z[:, t.parity, c, j * P:(j + 1) * P], ident[:])
                last.then_inc(z_ps, 1)

            pe.wait_ge(ident_ready, 1)
            pe.wait_ge(cond_in, 16)
            pe.transpose(ps_sum[:, 0:B], cond_sb[:], ident[0:B, 0:B])
            pe.wait_ge(vec_in, 32)
            pe.transpose(ps_sum[:, B:B + 2 * DC], vec_rows[:], ident[0:2 * DC, 0:2 * DC]).then_inc(condT_ps, 1)
            transpose_in(Tile(0, 0, 0))
            pe.wait_ge(condT_sb, 1)
            pe.wait_ge(dgb_in, 32)
            for g in range(2):
                for half in range(2):
                    last = pe.matmul(ps_y[half * H:(half + 1) * H, 1, g * B:(g + 1) * B], dgb_sb[:, g], condT[:],
                                     start=True, stop=True)
            last.then_inc(dtab_ps, 1)
            pe.wait_ge(aff_in, 16)
            for c in range(DC):
                last = pe.transpose(ps_up[:, 1, c * P:(c + 1) * P], aff_sb[:, c], ident[:])
            last.then_inc(affT_ps, 1)
            pe.wait_ge(ugb_in, 32)
            for g in range(2):
                for c in range(DC):
                    last = pe.matmul(ps_up[:, 0, (g * DC + c) * B:(g * DC + c + 1) * B],
                                     ugb_sb[:, g, c * P:(c + 1) * P], condT[:], start=True, stop=True)
            last.then_inc(utab_ps, 1)
            pe.wait_ge(affT_sb, 1)
            for c in range(DC):
                last = pe.matmul(ps_sum[:, c * B:(c + 1) * B], affT[:, c * P:(c + 1) * P], condT[:],
                                 start=True, stop=True)
            last.then_inc(style_ps, 1)

            def transpose_weight():
                pe.wait_ge(w_in, 16)
                for c in range(DC):
                    for o in range(DC):
                        last = pe.transpose(ps_y[:, 0, c * D + o * P:c * D + (o + 1) * P],
                                            w_sb[:, o, c * P:(c + 1) * P], ident[:])
                last.then_inc(wT_ps, 1)

            def norms():
                pe.wait_ge(wsq_ready, 1)
                pe.wait_ge(ssq_ready, 1)
                pe.wait_ge(dtab_sb, 1)
                for o in range(DC):
                    for c in range(DC):
                        last = pe.matmul(ps_y[:, 1, o * B:(o + 1) * B], wT_sq[:, c, o * P:(o + 1) * P],
                                         style_sq[:, c], start=(c == 0), stop=(c == DC - 1))
                last.then_inc(norm_ps, 1)

            def step(tile, first):
                if first == 0:
                    pe.wait_ge(dp_in, 16)
                    pe.wait_ge(ones_ready, 1)
                if tile(0):
                    down(tile(0))
                if first == 0:
                    transpose_weight()
                if tile(-1):
                    transpose_in(tile(-1))
                if first == 0:
                    norms()
                if first == 1:
                    pe.wait_ge(up_lo_ready, 1)
                    pe.wait_ge(utab_sb, 1)
                    pe.wait_ge(style_sb, 1)
                if tile(1):
                    up(tile(1))
                if first == 2:
                    pe.wait_ge(wT_sb, 1)
                    pe.wait_ge(norm_sb, 1)
                if tile(2):
                    for o in range(DC):
                        linear(tile(2), o)
                if tile(3):
                    transpose_out(tile(3))
            steps(pe, step)


_INS = ['x', 'cond_512', 'L0_cond_down_project', 'L0_cond_down_gamma', 'L0_cond_down_beta', 'L0_cond_up_project',
        'L0_cond_up_gamma', 'L0_cond_up_beta', 'L1_cond_weight', 'L1_cond_bias', 'L1_cond_affine_w',
        'L1_cond_affine_b']
_OUTS = [((64, 64, 256), 'float32')]


def kernel(**inputs):
    import numpy as _np
    import concourse.bacc as _bacc
    from concourse import mybir as _mybir
    from concourse.bass_utils import run_bass_kernel_spmd as _run

    nc = _bacc.Bacc("TRN2", target_bir_lowering=False, num_devices=1)
    arrays, args = {}, []
    for name in _INS:
        a = _np.ascontiguousarray(inputs[name])
        arrays[f"in_{name}_dram"] = a
        args.append(nc.dram_tensor(f"in_{name}_dram", a.shape, _mybir.dt.from_np(a.dtype), kind="ExternalInput").ap())
    for i, (shape, dtype) in enumerate(_OUTS):
        dt = _mybir.dt.from_np(_np.dtype(dtype))
        args.append(nc.dram_tensor(f"out_{i}_dram", shape, dt, kind="ExternalOutput").ap())
    bass_cond_resid(nc, *args)
    r = _run(nc, [arrays], core_ids=[0])
    return r.results[0]["out_0_dram"]
```

```python
from collections import namedtuple
from contextlib import ExitStack

import concourse.bass as bass
from concourse import mybir

ALU = mybir.AluOpType
ACT = mybir.ActivationFunctionType
F32 = mybir.dt.float32
F32R = mybir.dt.float32r

P = 128
Tile = namedtuple("Tile", "n parity half")
CLAMP = 256.0
EPS = 1e-8


def bass_cond_resid(nc, x, cond, down_project, down_gamma, down_beta, up_project, up_gamma, up_beta,
                    weight, bias, affine_w, affine_b, out):
    B, S, D = x.shape
    H = down_project.shape[1]
    C = cond.shape[1]
    DC = D // P
    T = 512
    TB = T // S
    TILES = B * S // T
    TJ = T // P
    HT = T // 2
    HB = TB // 2
    GAIN = float(C) ** -0.5
    WARM = 8
    assert H == P // 2 and C == P and DC == 2 and TILES >= 8 and TILES % 2 == 0

    x_tiles = x.rearrange("b s d -> (b s) d").rearrange("(t j p) d -> t p j d", p=P, j=TJ)
    out_tiles = out.rearrange("b s d -> (b s) d").rearrange("(t j p) d -> t p j d", p=P, j=TJ)

    with ExitStack() as ctx:
        def sb(name, shape, dt=F32):
            return ctx.enter_context(nc.sbuf_tensor(name, shape, dt))

        def psum(name, shape):
            return ctx.enter_context(nc.psum_tensor(name, shape, F32))

        def sem(name):
            return ctx.enter_context(nc.semaphore(name))

        ident = sb("ident", [P, P])
        ones = sb("ones", [P, H])
        ones_r = sb("ones_r", [P, P], F32R)
        cond_sb = sb("cond_sb", [B, C])
        condT = sb("condT", [C, B])
        dp_sb = sb("dp_sb", [P, DC, H])
        dgb_sb = sb("dgb_sb", [C, 2, H])
        up_sb = sb("up_sb", [P, D])
        up_hi = sb("up_hi", [P, D], F32R)
        up_lo = sb("up_lo", [P, D], F32R)
        ugb_sb = sb("ugb_sb", [C, 2, D])
        w_sb = sb("w_sb", [P, DC, D])
        wT = sb("wT", [P, DC, D])
        wT_sq = sb("wT_sq", [P, DC, D])
        aff_sb = sb("aff_sb", [P, DC, C])
        affT = sb("affT", [C, D])
        vec_rows = sb("vec_rows", [2 * DC, P])
        vec_cols = sb("vec_cols", [P, 2 * DC])
        down_tab = sb("down_tab", [P, 2, TILES, HB])
        up_tab = sb("up_tab", [P, 2, DC, B])
        style = sb("style", [P, DC, B])
        style_sq = sb("style_sq", [P, DC, B])
        demod = sb("demod", [P, DC, B])
        dm_q = sb("dm_q", [P, DC, B])
        dm_r = sb("dm_r", [P, DC, B])
        dm_t = sb("dm_t", [P, DC, B])

        x_nat = sb("x_nat", [P, 2, TJ, D])
        xT = sb("xT", [P, 2, DC, T])
        sum_sc = sb("sum_sc", [P, HT])
        act_hl = sb("act_hl", [P, 2, T], F32R)
        act_sum = sb("act_sum", [P, T])
        off_sc = sb("off_sc", [P, DC, T])
        x2 = sb("x2", [P, TILES, DC, T])
        xm = sb("xm", [P, 2, DC, T])
        z = sb("z", [P, 2, DC, T])
        out_nat = sb("out_nat", [P, TILES, TJ, D])

        ps_io = psum("ps_io", [P, 2 * T])
        ps_down = psum("ps_down", [P, 2, HT])
        pre = ps_down[:, 0]
        ps_sum = psum("ps_sum", [P, T])
        ps_up = psum("ps_up", [P, DC, T])
        ps_y = psum("ps_y", [P, DC, T])

        x_loaded = [sem(f"x_loaded{i}") for i in range(2)]
        out_stored = sem("out_stored")
        cond_in, dp_in, dgb_in, up_in = sem("cond_in"), sem("dp_in"), sem("dgb_in"), sem("up_in")
        ugb_in, w_in, aff_in, vec_in = sem("ugb_in"), sem("w_in"), sem("aff_in"), sem("vec_in")
        zeroed, ident_ready, ones_ready = sem("zeroed"), sem("ident_ready"), sem("ones_ready")
        condT_ps, condT_sb = sem("condT_ps"), sem("condT_sb")
        dtab_ps, dtab_sb = sem("dtab_ps"), sem("dtab_sb")
        utab_ps, utab_sb = sem("utab_ps"), sem("utab_sb")
        affT_ps, affT_sb = sem("affT_ps"), sem("affT_sb")
        wT_ps, wT_sb, wsq_ready = sem("wT_ps"), sem("wT_sb"), sem("wsq_ready")
        style_ps, style_sb, ssq_ready = sem("style_ps"), sem("style_sb"), sem("ssq_ready")
        norm_ps, norm_sb, root_done, newton = sem("norm_ps"), sem("norm_sb"), sem("root_done"), sem("newton")
        up_hi_ready, up_lo_ready = sem("up_hi_ready"), sem("up_lo_ready")

        xT_ps, xT_sb, x_doubled = sem("xT_ps"), sem("xT_sb"), sem("x_doubled")
        down_ps, down_scaled, pre_ready = sem("down_ps"), sem("down_scaled"), sem("pre_ready")
        hi_ready, lo_ready = sem("hi_ready"), sem("lo_ready")
        up_ps, up_scaled, off_scaled, off_added = sem("up_ps"), sem("up_scaled"), sem("off_scaled"), sem("off_added")
        act_sum_ready = sem("act_sum_ready")
        x2_ready = sem("x2_ready")
        xm_ready = sem("xm_ready")
        end_xm_ready = sem("end_xm_ready")
        end_off_scaled, end_off_added = sem("end_off_scaled"), sem("end_off_added")
        y_ps = [sem(f"y_ps{c}") for c in range(DC)]
        y_scaled = [sem(f"y_scaled{c}") for c in range(DC)]
        y_capped = [sem(f"y_capped{c}") for c in range(DC)]
        z_ready = [sem(f"z_ready{c}") for c in range(DC)]
        z_ps, out_ready = sem("z_ps"), sem("out_ready")

        FIRST = 3
        PAIRS = (TILES - 1 - FIRST) // 2

        def steps(eng, step):
            def peeled(k):
                def tile(lag):
                    n = k - lag
                    return Tile(n, n % 2, n // 2) if 0 <= n < TILES else None
                step(tile, k)

            for k in range(FIRST):
                peeled(k)
            with eng.Fori(0, PAIRS) as pair:
                for u in range(2):
                    def tile(lag):
                        k = FIRST + u - lag
                        return Tile(2 * pair + k, k % 2, pair + k // 2)
                    step(tile, None)
            for k in range(FIRST + 2 * PAIRS, TILES + 3):
                peeled(k)

        def wait(eng, s, count):
            if not isinstance(count, int) or count > 0:
                eng.wait_ge(s, count)

        def at_end(t):
            return isinstance(t.n, int) and t.n in (0, TILES - 1)

        def per_batch(table):
            return table.unsqueeze(3).to_broadcast([P, table.shape[1], table.shape[2], S])

        def by_batch(tile):
            return tile.rearrange("p c (b s) -> p c b s", s=S)

        block = ctx.enter_context(nc.Block())

        @block.sync
        def _(sp):
            def load(n, parity):
                wait(sp, xT_ps, n - 1)
                sp.dma_start(x_nat[:, parity], x_tiles[n]).then_inc(x_loaded[parity], 16)

            load(0, 0)
            sp.dma_start(cond_sb[:], cond).then_inc(cond_in, 16)
            sp.dma_start(dp_sb[:], down_project.rearrange("(c p) h -> p c h", p=P)).then_inc(dp_in, 16)
            sp.dma_start(dgb_sb[:, 0], down_gamma).then_inc(dgb_in, 16)
            sp.dma_start(dgb_sb[:, 1], down_beta).then_inc(dgb_in, 16)
            load(1, 1)
            with sp.Fori(1, TILES // 2) as pair:
                for parity in range(2):
                    load(2 * pair + parity, parity)
            with sp.Fori(0, TILES) as n:
                sp.wait_ge(out_ready, n + 2)
                sp.dma_start(out_tiles[n], out_nat[:, n]).then_inc(out_stored, 16)
            sp.wait_ge(out_stored, 16 * TILES)

        @block.scalar
        def _(act):
            act.wait_ge(condT_ps, 1)
            act.activation(condT[:], ps_sum[:, 0:B], ACT.Copy).then_inc(condT_sb, 1)
            act.sem_inc(out_ready, 1)

            def evacuate_xT(t):
                act.wait_ge(xT_ps, t.n + 1)
                wait(act, down_ps, t.n - 1)
                act.activation(xT[:, t.parity].rearrange("p c t -> p (c t)"), ps_io[:], ACT.Copy).then_inc(xT_sb, 1)

            def double(t):
                act.activation(x2[:, t.n].rearrange("p c t -> p (c t)"), ps_io[:], ACT.Copy,
                               scale=2.0).then_inc(x_doubled, 1)

            def relu_high(t):
                act.wait_ge(pre_ready, t.n + 1)
                wait(act, up_ps, t.n - 1)
                act.activation(act_hl[0:H, t.parity, 0:HT], pre[0:H], ACT.Relu)
                act.activation(act_hl[H:P, t.parity, HT:T], pre[H:P], ACT.Relu).then_inc(hi_ready, 1)

            def evacuate_sum(t):
                act.wait_ge(up_ps, t.n + 1)
                wait(act, off_scaled, t.n)
                act.activation(act_sum[:], ps_sum[:], ACT.Copy).then_inc(act_sum_ready, 1)

            def evacuate_out(t):
                act.wait_ge(z_ps, t.n + 1)
                act.activation(out_nat[:, t.n].rearrange("p j d -> p (j d)"), ps_io[:], ACT.Copy).then_inc(out_ready, 1)

            def weights():
                act.wait_ge(up_in, 32)
                act.activation(up_hi[:], up_sb[:], ACT.Copy).then_inc(up_hi_ready, 1)
                act.wait_ge(affT_ps, 1)
                act.activation(affT[:], ps_up[:, 1, 0:D], ACT.Copy)
                act.activation(vec_cols[:], ps_up[:, 1, D:D + 2 * DC], ACT.Copy).then_inc(affT_sb, 1)
                act.wait_ge(affT_sb, 1)
                act.wait_ge(style_ps, 1)
                for c in range(DC):
                    last = act.activation(style[:, c], ps_sum[:, c * B:(c + 1) * B], ACT.Identity,
                                          bias=vec_cols[:, c:c + 1], scale=GAIN)
                last.then_inc(style_sb, 1)

            def evacuate_weight():
                act.wait_ge(wT_ps, 1)
                act.activation(wT[:].rearrange("p c o -> p (c o)"), ps_y[:, 0], ACT.Copy).then_inc(wT_sb, 1)

            def root():
                act.wait_ge(norm_sb, 1)
                act.activation(dm_t[:], dm_q[:], ACT.Sqrt).then_inc(root_done, 1)

            def step(tile, first):
                if tile(-1):
                    evacuate_xT(tile(-1))
                if tile(1):
                    evacuate_sum(tile(1))
                if tile(0):
                    relu_high(tile(0))
                if first == 0:
                    weights()
                if first == 1:
                    evacuate_weight()
                if tile(-1):
                    double(tile(-1))
                if first == 2:
                    root()
                if tile(3):
                    evacuate_out(tile(3))
            evacuate_xT(Tile(0, 0, 0))
            double(Tile(0, 0, 0))
            steps(act, step)

        @block.vector
        def _(dve):
            dve.memset(ones[:], 1.0)
            dve.memset(ones_r[:].bitcast(F32), 1.0).then_inc(ones_ready, 1)

            dve.wait_ge(dtab_ps, 1)
            for g in range(2):
                for half in range(2):
                    rows = slice(half * H, (half + 1) * H)
                    src = ps_y[rows, 1, g * B:(g + 1) * B].rearrange("p (t b) -> p t b", b=TB)
                    last = dve.tensor_copy(down_tab[rows, g], src[:, :, half * HB:(half + 1) * HB])
            last.then_inc(dtab_sb, 1)

            def tables():
                dve.wait_ge(up_hi_ready, 1)
                dve.tensor_tensor(up_lo[:], up_sb[:], up_hi[:].bitcast(F32), ALU.subtract).then_inc(up_lo_ready, 1)
                dve.wait_ge(utab_ps, 1)
                dve.tensor_copy(up_tab[:].rearrange("p g c b -> p (g c b)"), ps_up[:, 0, 0:2 * DC * B]).then_inc(utab_sb, 1)
                dve.wait_ge(style_sb, 1)
                dve.tensor_tensor(style_sq[:], style[:], style[:], ALU.mult).then_inc(ssq_ready, 1)
                dve.wait_ge(utab_sb, 1)

            def squares():
                dve.wait_ge(wT_sb, 1)
                dve.tensor_tensor(wT_sq[:], wT[:], wT[:], ALU.mult).then_inc(wsq_ready, 1)

            def norm():
                dve.wait_ge(norm_ps, 1)
                dve.tensor_scalar(dm_q[:].rearrange("p c b -> p (c b)"), ps_y[:, 1, 0:DC * B], EPS, None,
                                  ALU.add).then_inc(norm_sb, 1)

            def demodulation():

                dve.wait_ge(root_done, 1)
                dve.reciprocal(dm_r[:], dm_t[:]).then_inc(newton, 1)
                dve.wait_ge(newton, 1)
                dve.tensor_tensor(dm_t[:], dm_r[:], dm_r[:], ALU.mult).then_inc(newton, 1)
                dve.wait_ge(newton, 2)
                dve.tensor_tensor(dm_q[:], dm_t[:], dm_q[:], ALU.mult).then_inc(newton, 1)
                dve.wait_ge(newton, 3)
                dve.tensor_scalar(dm_t[:], dm_q[:], -0.5, 1.5, ALU.mult, ALU.add).then_inc(newton, 1)
                dve.wait_ge(newton, 4)
                dve.tensor_tensor(demod[:], dm_t[:], dm_r[:], ALU.mult).then_inc(newton, 1)
                dve.wait_ge(newton, 5)

            def scale_down(t):
                dve.wait_ge(down_ps, t.n + 1)
                wait(dve, pre_ready, t.n)
                for g, scaled in ((1, sum_sc[:]), (0, pre)):
                    tab = down_tab[:, g, t.n, :].unsqueeze(2).to_broadcast([P, HB, S])
                    last = dve.tensor_tensor(scaled.rearrange("p (b s) -> p b s", s=S),
                                             ps_down[:, g].rearrange("p (b s) -> p b s", s=S), tab, ALU.mult)
                last.then_inc(down_scaled, 1)

            def sum_down(t):
                dve.wait_ge(down_scaled, t.n + 1)
                dve.tensor_tensor(pre, pre, sum_sc[:], ALU.add).then_inc(pre_ready, 1)

            def relu_low(t):
                dve.wait_ge(hi_ready, t.n + 1)
                dve.scalar_tensor_tensor(out=act_hl[H:P, t.parity, 0:HT], in0=pre[0:H], scalar=0.0,
                                         in1=act_hl[0:H, t.parity, 0:HT].bitcast(F32), op0=ALU.max, op1=ALU.subtract)
                dve.scalar_tensor_tensor(out=act_hl[0:H, t.parity, HT:T], in0=pre[H:P], scalar=0.0,
                                         in1=act_hl[H:P, t.parity, HT:T].bitcast(F32), op0=ALU.max,
                                         op1=ALU.subtract).then_inc(lo_ready, 1)

            def scale_up(t):
                dve.wait_ge(up_ps, t.n + 1)
                dve.tensor_tensor(by_batch(ps_up[:]), by_batch(ps_up[:]), per_batch(up_tab[:, 0, :, bass.ds(t.n * TB, TB)]),
                                  ALU.mult).then_inc(up_scaled, 1)

            def offset_share(t):
                count = 1 if t.n == 0 else 2
                dve.wait_ge(act_sum_ready, t.n + 1)
                dve.tensor_tensor(ps_sum[:].rearrange("p (b s) -> p b s", s=S),
                                  ps_sum[:].rearrange("p (b s) -> p b s", s=S),
                                  up_tab[:, 1, 1, t.n * TB:(t.n + 1) * TB].unsqueeze(2).to_broadcast([P, TB, S]),
                                  ALU.mult).then_inc(end_off_scaled, 1)
                dve.wait_ge(end_off_scaled, count)
                dve.wait_ge(x_doubled, t.n + 1)
                dve.tensor_tensor(x2[:, t.n, 1], ps_sum[:], x2[:, t.n, 1], ALU.add).then_inc(end_off_added, 1)
                dve.wait_ge(end_off_added, count)

            def modulate(t):
                dve.wait_ge(style_sb, 1)
                dve.wait_ge(x2_ready, t.n + 1)
                wait(dve, y_ps[DC - 1], t.n - 1)
                dve.tensor_tensor(by_batch(xm[:, t.parity]), by_batch(x2[:, t.n]),
                                  per_batch(style[:, :, t.n * TB:(t.n + 1) * TB]), ALU.mult).then_inc(end_xm_ready, 1)

            def residual(t):
                dve.wait_ge(up_scaled, t.n + 1)
                dve.wait_ge(off_added, t.n + 1)
                dve.tensor_tensor(x2[:, t.n], ps_up[:], x2[:, t.n], ALU.add).then_inc(x2_ready, 1)

            def demodulate(t, c):
                dve.wait_ge(y_ps[c], t.n + 1)
                tab = demod[:, c, bass.ds(t.n * TB, TB)].unsqueeze(2).to_broadcast([P, TB, S])
                dve.tensor_tensor(ps_y[:, c].rearrange("p (b s) -> p b s", s=S),
                                  ps_y[:, c].rearrange("p (b s) -> p b s", s=S), tab, ALU.mult).then_inc(y_scaled[c], 1)

            def cap(t, c):
                dve.wait_ge(y_scaled[c], t.n + 1)
                dve.tensor_scalar(ps_y[:, c], ps_y[:, c], vec_cols[:, DC + c:DC + c + 1], CLAMP, ALU.add,
                                  ALU.min).then_inc(y_capped[c], 1)

            def finish(t, c):
                dve.wait_ge(y_capped[c], t.n + 1)
                dve.scalar_tensor_tensor(out=z[:, t.parity, c], in0=ps_y[:, c], scalar=-CLAMP, in1=x2[:, t.n, c],
                                         op0=ALU.max, op1=ALU.add).then_inc(z_ready[c], 1)

            def step(tile, first):
                if first == 0:
                    dve.wait_ge(dtab_sb, 1)
                if tile(3):
                    demodulate(tile(3), 1)
                if tile(0):
                    scale_down(tile(0))
                if tile(3):
                    cap(tile(3), 1)
                if tile(0):
                    sum_down(tile(0))
                if tile(3):
                    finish(tile(3), 1)
                if first == 2:
                    norm()
                if tile(0):
                    relu_low(tile(0))
                if first == 0:
                    tables()
                if tile(1):
                    scale_up(tile(1))
                    if at_end(tile(1)):
                        offset_share(tile(1))
                        residual(tile(1))
                        modulate(tile(1))
                if first == 1:
                    squares()
                if first == 2:
                    residual(tile(1))
                    demodulation()
                if tile(2):
                    demodulate(tile(2), 0)
                if tile(1) and not at_end(tile(1)) and first != 2:
                    residual(tile(1))
                if tile(2):
                    cap(tile(2), 0)
                    finish(tile(2), 0)
            steps(dve, step)

        @block.gpsimd
        def _(pool):
            pool.memset(ident[:], 0.0).then_inc(zeroed, 1)
            pool.wait_ge(zeroed, 1)
            pool.affine_select(out=ident[:], in_=ident[:], compare_op=ALU.not_equal, fill=1.0, base=0,
                               pattern=[[-1, P]], channel_multiplier=1).then_inc(ident_ready, 1)
            pool.dma_start(aff_sb[:], affine_w.rearrange("(c p) w -> p c w", p=P)).then_inc(aff_in, 16)
            pool.dma_start(vec_rows[0:DC], affine_b.rearrange("(c p) -> c p", p=P)).then_inc(vec_in, 16)
            pool.dma_start(vec_rows[DC:2 * DC], bias.rearrange("(c p) -> c p", p=P)).then_inc(vec_in, 16)
            pool.dma_start(up_sb[0:H, :], up_project).then_inc(up_in, 16)
            pool.dma_start(up_sb[H:P, :], up_project).then_inc(up_in, 16)
            pool.dma_start(ugb_sb[:, 0], up_gamma).then_inc(ugb_in, 16)
            pool.dma_start(ugb_sb[:, 1], up_beta).then_inc(ugb_in, 16)
            pool.dma_start(w_sb[:], weight.rearrange("(o p) c -> p o c", p=P)).then_inc(w_in, 16)

            def offset(t):
                pool.wait_ge(act_sum_ready, t.n + 1)
                wait(pool, off_added, t.n)
                chunks = 1 if at_end(t) else DC
                sums = by_batch(act_sum[:].unsqueeze(1).to_broadcast([P, chunks, T]))
                pool.tensor_tensor(by_batch(off_sc[:, 0:chunks]), sums,
                                   per_batch(up_tab[:, 1, 0:chunks, bass.ds(t.n * TB, TB)]),
                                   ALU.mult).then_inc(off_scaled, 1)
                pool.wait_ge(off_scaled, t.n + 1)
                pool.wait_ge(x_doubled, t.n + 1)
                pool.tensor_tensor(x2[:, t.n, 0:chunks], x2[:, t.n, 0:chunks], off_sc[:, 0:chunks], ALU.add).then_inc(off_added, 1)

            def modulate(t):
                pool.wait_ge(x2_ready, t.n + 1)
                wait(pool, y_ps[DC - 1], t.n - 1)
                pool.tensor_tensor(by_batch(xm[:, t.parity]), by_batch(x2[:, t.n]),
                                   per_batch(style[:, :, bass.ds(t.n * TB, TB)]), ALU.mult).then_inc(xm_ready, 1)

            def step(tile, first):
                if tile(1):
                    if first == 1:
                        pool.wait_ge(utab_sb, 1)
                        pool.wait_ge(style_sb, 1)
                    offset(tile(1))
                    if not at_end(tile(1)):
                        modulate(tile(1))
            steps(pool, step)

        @block.tensor
        def _(pe):
            def transpose_in(t):
                pe.wait_ge(x_loaded[t.parity], 16 * (t.half + 1))
                wait(pe, x_doubled, t.n)
                wait(pe, out_ready, t.n - 3)
                for c in range(DC):
                    for j in range(TJ):
                        last = pe.transpose(ps_io[:, c * T + j * P:c * T + (j + 1) * P],
                                            x_nat[:, t.parity, j, c * P:(c + 1) * P], ident[:])
                last.then_inc(xT_ps, 1)

            def down(t):
                pe.wait_ge(xT_sb, t.n + 1)
                wait(pe, hi_ready, t.n)
                wait(pe, lo_ready, t.n)
                for g in range(2):
                    for c in range(DC):
                        for half in range(2):
                            last = pe.matmul(ps_down[half * H:(half + 1) * H, g],
                                             dp_sb[:, c] if g == 0 else ones[:],
                                             xT[:, t.parity, c, half * HT:(half + 1) * HT],
                                             start=(c == 0), stop=(c == DC - 1))
                last.then_inc(down_ps, 1)

            def up(t):
                pe.wait_ge(hi_ready, t.n + 1)
                pe.wait_ge(lo_ready, t.n + 1)
                wait(pe, x2_ready, t.n)
                wait(pe, act_sum_ready, t.n)
                if isinstance(t.n, int) and t.n == 1:
                    pe.wait_ge(end_off_added, 1)
                for c in range(DC):
                    pe.matmul(ps_up[:, c], up_hi[:, c * P:(c + 1) * P], act_hl[:, t.parity], start=True, stop=False)
                    pe.matmul(ps_up[:, c], up_lo[:, c * P:(c + 1) * P], act_hl[:, t.parity], start=False, stop=True)
                pe.matmul(ps_sum[:], ones_r[:], act_hl[:, t.parity], start=True, stop=True).then_inc(up_ps, 1)

            def linear(t, o):
                if at_end(t):
                    pe.wait_ge(end_xm_ready, 1 if t.n == 0 else 2)
                else:
                    pe.wait_ge(xm_ready, t.n)
                wait(pe, z_ready[o], t.n)
                for c in range(DC):
                    last = pe.matmul(ps_y[:, o], wT[:, c, o * P:(o + 1) * P], xm[:, t.parity, c],
                                     start=(c == 0), stop=(c == DC - 1))
                last.then_inc(y_ps[o], 1)

            def transpose_out(t):
                pe.wait_ge(x_doubled, min(t.n + 5, TILES) if isinstance(t.n, int) else t.n + 5)
                pe.wait_ge(out_ready, t.n + 1)
                for c in range(DC):
                    pe.wait_ge(z_ready[c], t.n + 1)
                    for j in range(TJ):
                        last = pe.transpose(ps_io[:, j * D + c * P:j * D + (c + 1) * P],
                                            z[:, t.parity, c, j * P:(j + 1) * P], ident[:])
                last.then_inc(z_ps, 1)

            pe.wait_ge(ident_ready, 1)
            for _ in range(WARM):
                pe.matmul(ps_y[:, 0, 0:P], ident[:], ident[:], start=True, stop=True)
            pe.wait_ge(cond_in, 16)
            pe.transpose(ps_sum[:, 0:B], cond_sb[:], ident[0:B, 0:B]).then_inc(condT_ps, 1)
            transpose_in(Tile(0, 0, 0))
            pe.wait_ge(condT_sb, 1)
            pe.wait_ge(dgb_in, 32)
            for g in range(2):
                for half in range(2):
                    last = pe.matmul(ps_y[half * H:(half + 1) * H, 1, g * B:(g + 1) * B], dgb_sb[:, g], condT[:],
                                     start=True, stop=True)
            last.then_inc(dtab_ps, 1)

            def tables():
                pe.wait_ge(aff_in, 16)
                pe.wait_ge(vec_in, 32)
                for c in range(DC):
                    pe.transpose(ps_up[:, 1, c * P:(c + 1) * P], aff_sb[:, c], ident[:])
                pe.transpose(ps_up[:, 1, D:D + 2 * DC], vec_rows[:], ident[0:2 * DC, 0:2 * DC]).then_inc(affT_ps, 1)
                pe.wait_ge(ugb_in, 32)
                for g in range(2):
                    for c in range(DC):
                        last = pe.matmul(ps_up[:, 0, (g * DC + c) * B:(g * DC + c + 1) * B],
                                         ugb_sb[:, g, c * P:(c + 1) * P], condT[:], start=True, stop=True)
                last.then_inc(utab_ps, 1)
                pe.wait_ge(affT_sb, 1)
                for c in range(DC):
                    last = pe.matmul(ps_sum[:, c * B:(c + 1) * B], affT[:, c * P:(c + 1) * P], condT[:],
                                     start=True, stop=True)
                last.then_inc(style_ps, 1)

            def transpose_weight():
                pe.wait_ge(w_in, 16)
                for c in range(DC):
                    for o in range(DC):
                        last = pe.transpose(ps_y[:, 0, c * D + o * P:c * D + (o + 1) * P],
                                            w_sb[:, o, c * P:(c + 1) * P], ident[:])
                last.then_inc(wT_ps, 1)

            def norms():
                pe.wait_ge(wsq_ready, 1)
                pe.wait_ge(ssq_ready, 1)
                pe.wait_ge(dtab_sb, 1)
                for o in range(DC):
                    for c in range(DC):
                        last = pe.matmul(ps_y[:, 1, o * B:(o + 1) * B], wT_sq[:, c, o * P:(o + 1) * P],
                                         style_sq[:, c], start=(c == 0), stop=(c == DC - 1))
                last.then_inc(norm_ps, 1)

            def step(tile, first):
                if first == 0:
                    pe.wait_ge(dp_in, 16)
                    pe.wait_ge(ones_ready, 1)
                if tile(0):
                    down(tile(0))
                if first == 0:
                    transpose_in(tile(-1))
                    tables()
                elif tile(-1):
                    transpose_in(tile(-1))
                if first == 1:
                    pe.wait_ge(up_lo_ready, 1)
                    pe.wait_ge(utab_sb, 1)
                    pe.wait_ge(style_sb, 1)
                if tile(1):
                    up(tile(1))
                if first == 1:
                    transpose_weight()
                if first == 2:
                    norms()
                if first == 2:
                    pe.wait_ge(wT_sb, 1)
                    pe.wait_ge(norm_sb, 1)
                if tile(2):
                    for o in range(DC):
                        linear(tile(2), o)
                if tile(3):
                    transpose_out(tile(3))
            steps(pe, step)


_INS = ['x', 'cond_512', 'L0_cond_down_project', 'L0_cond_down_gamma', 'L0_cond_down_beta', 'L0_cond_up_project',
        'L0_cond_up_gamma', 'L0_cond_up_beta', 'L1_cond_weight', 'L1_cond_bias', 'L1_cond_affine_w',
        'L1_cond_affine_b']
_OUTS = [((64, 64, 256), 'float32')]


def kernel(**inputs):
    import numpy as _np
    import concourse.bacc as _bacc
    from concourse import mybir as _mybir
    from concourse.bass_utils import run_bass_kernel_spmd as _run

    nc = _bacc.Bacc("TRN2", target_bir_lowering=False, num_devices=1)
    arrays, args = {}, []
    for name in _INS:
        a = _np.ascontiguousarray(inputs[name])
        arrays[f"in_{name}_dram"] = a
        args.append(nc.dram_tensor(f"in_{name}_dram", a.shape, _mybir.dt.from_np(a.dtype), kind="ExternalInput").ap())
    for i, (shape, dtype) in enumerate(_OUTS):
        dt = _mybir.dt.from_np(_np.dtype(dtype))
        args.append(nc.dram_tensor(f"out_{i}_dram", shape, dt, kind="ExternalOutput").ap())
    bass_cond_resid(nc, *args)
    r = _run(nc, [arrays], core_ids=[0])
    return r.results[0]["out_0_dram"]
```

```python
from collections import namedtuple
from contextlib import ExitStack

import concourse.bass as bass
from concourse import mybir

ALU = mybir.AluOpType
ACT = mybir.ActivationFunctionType
F32 = mybir.dt.float32
F32R = mybir.dt.float32r

P = 128
Tile = namedtuple("Tile", "n parity half")
CLAMP = 256.0
EPS = 1e-8


def bass_cond_resid(nc, x, cond, down_project, down_gamma, down_beta, up_project, up_gamma, up_beta,
                    weight, bias, affine_w, affine_b, out):
    B, S, D = x.shape
    H = down_project.shape[1]
    C = cond.shape[1]
    DC = D // P
    T = 512
    TB = T // S
    TILES = B * S // T
    TJ = T // P
    HT = T // 2
    HB = TB // 2
    GAIN = float(C) ** -0.5
    WARM = 6
    assert H == P // 2 and C == P and DC == 2 and TILES >= 8 and TILES % 2 == 0

    x_tiles = x.rearrange("b s d -> (b s) d").rearrange("(t j p) d -> t p j d", p=P, j=TJ)
    out_tiles = out.rearrange("b s d -> (b s) d").rearrange("(t j p) d -> t p j d", p=P, j=TJ)

    with ExitStack() as ctx:
        def sb(name, shape, dt=F32):
            return ctx.enter_context(nc.sbuf_tensor(name, shape, dt))

        def psum(name, shape):
            return ctx.enter_context(nc.psum_tensor(name, shape, F32))

        def sem(name):
            return ctx.enter_context(nc.semaphore(name))

        ident = sb("ident", [P, P])
        ones = sb("ones", [P, H])
        ones_r = sb("ones_r", [P, P], F32R)
        cond_sb = sb("cond_sb", [B, C])
        condT = sb("condT", [C, B])
        dp_sb = sb("dp_sb", [P, DC, H])
        dgb_sb = sb("dgb_sb", [C, 2, H])
        up_sb = sb("up_sb", [P, D])
        up_hi = sb("up_hi", [P, D], F32R)
        up_lo = sb("up_lo", [P, D], F32R)
        ugb_sb = sb("ugb_sb", [C, 2, D])
        w_sb = sb("w_sb", [P, DC, D])
        wT = sb("wT", [P, DC, D])
        wT_sq = sb("wT_sq", [P, DC, D])
        aff_sb = sb("aff_sb", [P, DC, C])
        affT = sb("affT", [C, D])
        vec_rows = sb("vec_rows", [2 * DC, P])
        vec_cols = sb("vec_cols", [P, 2 * DC])
        down_tab = sb("down_tab", [P, 2, TILES, HB])
        up_tab = sb("up_tab", [P, 2, DC, B])
        style = sb("style", [P, DC, B])
        style_sq = sb("style_sq", [P, DC, B])
        demod = sb("demod", [P, DC, B])
        dm_q = sb("dm_q", [P, DC, B])
        dm_r = sb("dm_r", [P, DC, B])
        dm_t = sb("dm_t", [P, DC, B])

        x_nat = sb("x_nat", [P, 2, TJ, D])
        xT = sb("xT", [P, 2, DC, T])
        sum_sc = sb("sum_sc", [P, HT])
        act_hl = sb("act_hl", [P, 2, T], F32R)
        act_sum = sb("act_sum", [P, T])
        off_sc = sb("off_sc", [P, DC, T])
        x2 = sb("x2", [P, TILES, DC, T])
        xm = sb("xm", [P, 2, DC, T])
        z = sb("z", [P, 2, DC, T])
        out_nat = sb("out_nat", [P, TILES, TJ, D])

        ps_io = psum("ps_io", [P, 2 * T])
        ps_down = psum("ps_down", [P, 2, HT])
        ps_sum = psum("ps_sum", [P, T])
        ps_up = psum("ps_up", [P, DC, T])
        ps_y = psum("ps_y", [P, DC, T])

        first_x_loaded = [sem(f"first_x_loaded{i}") for i in range(2)]
        x_loaded = [sem(f"x_loaded{i}") for i in range(2)]
        out_stored = sem("out_stored")
        cond_in, dp_in, dgb_in, up_in = sem("cond_in"), sem("dp_in"), sem("dgb_in"), sem("up_in")
        ugb_in, w_in, aff_in, vec_in = sem("ugb_in"), sem("w_in"), sem("aff_in"), sem("vec_in")
        zeroed, ident_ready, ones_ready = sem("zeroed"), sem("ident_ready"), sem("ones_ready")
        condT_ps, condT_sb = sem("condT_ps"), sem("condT_sb")
        dtab_ps, dtab_sb = sem("dtab_ps"), sem("dtab_sb")
        utab_ps, utab_sb = sem("utab_ps"), sem("utab_sb")
        affT_ps, affT_sb = sem("affT_ps"), sem("affT_sb")
        wT_ps, wT_sb, wsq_ready = sem("wT_ps"), sem("wT_sb"), sem("wsq_ready")
        style_ps, style_sb, ssq_ready = sem("style_ps"), sem("style_sb"), sem("ssq_ready")
        norm_ps, norm_ready, root_done, newton = sem("norm_ps"), sem("norm_ready"), sem("root_done"), sem("newton")
        up_hi_ready, up_lo_ready = sem("up_hi_ready"), sem("up_lo_ready")

        xT_ps, xT_sb, x_doubled = sem("xT_ps"), sem("xT_sb"), sem("x_doubled")
        first_xT_ps, first_xT_sb = sem("first_xT_ps"), sem("first_xT_sb")
        down_ps, down_scaled, pre_ready = sem("down_ps"), sem("down_scaled"), sem("pre_ready")
        hi_ready, lo_ready = sem("hi_ready"), sem("lo_ready")
        up_ps, up_scaled, up_added, act_sum_ready = sem("up_ps"), sem("up_scaled"), sem("up_added"), sem("act_sum_ready")
        off_scaled, x2_ready, xm_ready = sem("off_scaled"), sem("x2_ready"), sem("xm_ready")
        end_off_scaled, end_x2_ready, end_xm_ready = sem("end_off_scaled"), sem("end_x2_ready"), sem("end_xm_ready")
        y_ps = [sem(f"y_ps{c}") for c in range(DC)]
        y_scaled = [sem(f"y_scaled{c}") for c in range(DC)]
        y_capped = [sem(f"y_capped{c}") for c in range(DC)]
        z_ready = [sem(f"z_ready{c}") for c in range(DC)]
        last_z_ready = [sem(f"last_z_ready{c}") for c in range(DC)]
        z_ps, out_ready = sem("z_ps"), sem("out_ready")

        FIRST = 3
        PAIRS = (TILES - 1 - FIRST) // 2
        LAST = TILES - 1
        assert FIRST + 2 * PAIRS == LAST

        def at(n):
            return Tile(n, n % 2, n // 2)

        def steady(eng, step):
            with eng.Fori(0, PAIRS) as pair:
                for u in range(2):
                    def tile(lag):
                        k = FIRST + u - lag
                        return Tile(2 * pair + k, k % 2, pair + k // 2)
                    step(tile)

        def wait(eng, s, count):
            if not isinstance(count, int) or count > 0:
                eng.wait_ge(s, count)

        def shared(t):
            return isinstance(t.n, int) and t.n >= TILES - 2

        def shares(t):
            return t.n - (TILES - 3)

        def per_batch(table):
            return table.unsqueeze(3).to_broadcast([P, table.shape[1], table.shape[2], S])

        def by_batch(tile):
            return tile.rearrange("p c (b s) -> p c b s", s=S)

        def chunk_by_batch(chunk):
            return chunk.rearrange("p (b s) -> p b s", s=S)

        def chunk_per_batch(table):
            return table.unsqueeze(2).to_broadcast([P, table.shape[1], S])

        def down_bank(t):
            if isinstance(t.n, int) and t.n == 1:
                return ps_y[:, 1].rearrange("p (g t) -> p g t", g=2)
            return ps_down[:]

        def y_bank(t, c):
            if isinstance(t.n, int) and t.n == LAST:
                return ps_down[:].rearrange("p g t -> p (g t)") if c == 0 else ps_sum[:]
            return ps_y[:, c]

        block = ctx.enter_context(nc.Block())

        @block.sync
        def _(sp):
            def load(n, parity):
                wait(sp, xT_ps, n - 1)
                sp.dma_start(x_nat[:, parity], x_tiles[n]).then_inc(x_loaded[parity], 16)

            def load_first(half):
                blocks = slice(half * TJ // 2, (half + 1) * TJ // 2)
                sp.dma_start(x_nat[:, 0, blocks], x_tiles[0][:, blocks]).then_inc(first_x_loaded[half], 16)

            load_first(0)
            load_first(1)
            sp.dma_start(cond_sb[:], cond).then_inc(cond_in, 16)
            sp.dma_start(dp_sb[:], down_project.rearrange("(c p) h -> p c h", p=P)).then_inc(dp_in, 16)
            load(1, 1)
            sp.dma_start(w_sb[:], weight.rearrange("(o p) c -> p o c", p=P)).then_inc(w_in, 16)
            with sp.Fori(1, TILES // 2) as pair:
                for parity in range(2):
                    load(2 * pair + parity, parity)
            with sp.Fori(0, LAST) as n:
                sp.wait_ge(out_ready, n + 2)
                sp.dma_start(out_tiles[n], out_nat[:, n]).then_inc(out_stored, 16)
            for part in range(2):
                sp.wait_ge(out_ready, TILES + 1 + part)
                blocks = slice(part * TJ // 2, (part + 1) * TJ // 2)
                sp.dma_start(out_tiles[LAST][:, blocks], out_nat[:, LAST, blocks]).then_inc(out_stored, 16)
            sp.wait_ge(out_stored, 16 * (TILES + 1))

        @block.scalar
        def _(act):
            act.wait_ge(ones_ready, 1)
            act.activation(dm_t[:, 0, 0:1], ones[:, 0:1], ACT.Sqrt)
            act.dma_start(dgb_sb[:, 0], down_gamma).then_inc(dgb_in, 16)
            act.dma_start(dgb_sb[:, 1], down_beta).then_inc(dgb_in, 16)
            act.dma_start(ugb_sb[:, 0], up_gamma).then_inc(ugb_in, 16)
            act.dma_start(ugb_sb[:, 1], up_beta).then_inc(ugb_in, 16)

            act.sem_inc(out_ready, 1)

            def evacuate_xT(t):
                act.wait_ge(xT_ps, t.n + 1)
                wait(act, down_ps, t.n - 1)
                act.activation(xT[:, t.parity].rearrange("p c t -> p (c t)"), ps_io[:], ACT.Copy).then_inc(xT_sb, 1)

            def double(t):
                act.activation(x2[:, t.n].rearrange("p c t -> p (c t)"), ps_io[:], ACT.Copy,
                               scale=2.0).then_inc(x_doubled, 1)

            def relu_high(t):
                act.wait_ge(pre_ready, t.n + 1)
                wait(act, up_ps, t.n - 1)
                pre = down_bank(t)[:, 0]
                act.activation(act_hl[0:H, t.parity, 0:HT], pre[0:H], ACT.Relu)
                act.activation(act_hl[H:P, t.parity, HT:T], pre[H:P], ACT.Relu).then_inc(hi_ready, 1)

            def evacuate_sum(t):
                act.wait_ge(up_ps, t.n + 1)
                wait(act, off_scaled, t.n)
                act.activation(act_sum[:], ps_sum[:], ACT.Copy).then_inc(act_sum_ready, 1)

            def evacuate_out(t):
                act.wait_ge(z_ps, t.n + 1)
                act.activation(out_nat[:, t.n].rearrange("p j d -> p (j d)"), ps_io[:], ACT.Copy).then_inc(out_ready, 1)

            def evacuate_last(part):
                act.wait_ge(z_ps, TILES + part)
                act.activation(out_nat[:, LAST, part * TJ // 2:(part + 1) * TJ // 2].rearrange("p j d -> p (j d)"),
                               ps_io[:, part * T:(part + 1) * T], ACT.Copy).then_inc(out_ready, 1)

            def styles():
                act.wait_ge(affT_sb, 1)
                act.wait_ge(style_ps, 1)
                for c in range(DC):
                    last = act.activation(style[:, c], ps_sum[:, c * B:(c + 1) * B], ACT.Identity,
                                          bias=vec_cols[:, c:c + 1], scale=GAIN)
                last.then_inc(style_sb, 1)

            def evacuate_weight():
                act.wait_ge(wT_ps, 1)
                act.activation(wT[:].rearrange("p c o -> p (c o)"), ps_y[:, 0], ACT.Copy).then_inc(wT_sb, 1)

            def root():
                act.wait_ge(norm_ready, 1)
                act.activation(dm_t[:], dm_q[:], ACT.Sqrt).then_inc(root_done, 1)

            def demodulate(t, c):
                act.wait_ge(y_ps[c], t.n + 1)
                for b in range(TB):
                    tokens = ps_y[:, c, b * S:(b + 1) * S]
                    last = act.activation(tokens, tokens, ACT.Identity, bias=vec_cols[:, DC + c:DC + c + 1],
                                          scale=demod[:, c, bass.ds(t.n * TB + b, 1)])
                last.then_inc(y_scaled[c], 1)

            for half, transposed in enumerate((first_xT_ps, xT_ps)):
                act.wait_ge(transposed, 1)
                act.activation(xT[:, 0, :, half * HT:(half + 1) * HT],
                               ps_io[:, half * T:(half + 1) * T].rearrange("p (c t) -> p c t", c=DC),
                               ACT.Copy).then_inc(first_xT_sb, 1)
                if half == 0:
                    act.wait_ge(condT_ps, 1)
                    act.activation(condT[:], ps_sum[:, 0:B], ACT.Copy).then_inc(condT_sb, 1)
            act.wait_ge(affT_ps, 1)
            act.activation(affT[:], ps_up[:, 1, 0:D], ACT.Copy)
            act.activation(vec_cols[:], ps_up[:, 1, D:D + 2 * DC], ACT.Copy).then_inc(affT_sb, 1)
            for half in range(2):
                last = act.activation(x2[:, 0, :, half * HT:(half + 1) * HT],
                                      ps_io[:, half * T:(half + 1) * T].rearrange("p (c t) -> p c t", c=DC),
                                      ACT.Copy, scale=2.0)
            last.then_inc(x_doubled, 1)
            act.wait_ge(up_in, 32)
            act.activation(up_hi[:], up_sb[:], ACT.Copy).then_inc(up_hi_ready, 1)

            evacuate_weight()
            evacuate_xT(at(1))
            relu_high(at(0))
            double(at(1))
            styles()

            evacuate_xT(at(2))
            relu_high(at(1))
            evacuate_sum(at(0))
            double(at(2))
            root()

            evacuate_xT(at(3))
            relu_high(at(2))
            evacuate_sum(at(1))
            double(at(3))
            act.wait_ge(newton, 5)

            def step(tile):
                evacuate_sum(tile(1))
                evacuate_xT(tile(-1))
                relu_high(tile(0))
                double(tile(-1))
                demodulate(tile(2), 0)
                evacuate_out(tile(3))
            steady(act, step)

            evacuate_sum(at(LAST - 1))
            relu_high(at(LAST))
            demodulate(at(LAST - 2), 0)
            demodulate(at(LAST - 2), 1)
            evacuate_sum(at(LAST))
            evacuate_out(at(LAST - 3))
            demodulate(at(LAST - 1), 0)
            demodulate(at(LAST - 1), 1)
            evacuate_out(at(LAST - 2))
            evacuate_out(at(LAST - 1))
            for part in range(2):
                evacuate_last(part)

        @block.vector
        def _(dve):
            dve.memset(ones[:], 1.0)
            dve.memset(ones_r[:].bitcast(F32), 1.0).then_inc(ones_ready, 1)

            dve.wait_ge(dtab_ps, 1)
            for g in range(2):
                for half in range(2):
                    rows = slice(half * H, (half + 1) * H)
                    src = ps_y[rows, 1, g * B:(g + 1) * B].rearrange("p (t b) -> p t b", b=TB)
                    last = dve.tensor_copy(down_tab[rows, g], src[:, :, half * HB:(half + 1) * HB])
            last.then_inc(dtab_sb, 1)

            def tables():
                dve.wait_ge(utab_ps, 1)
                dve.tensor_copy(up_tab[:].rearrange("p g c b -> p (g c b)"), ps_up[:, 0, 0:2 * DC * B]).then_inc(utab_sb, 1)
                dve.wait_ge(utab_sb, 1)

            def add_eps():
                dve.wait_ge(norm_ps, 1)
                dve.tensor_scalar(dm_q[:].rearrange("p c b -> p (c b)"), ps_y[:, 0, 0:DC * B], EPS, None,
                                  ALU.add).then_inc(norm_ready, 1)

            def reciprocal():
                dve.wait_ge(root_done, 1)
                dve.reciprocal(dm_r[:], dm_t[:]).then_inc(newton, 1)

            def newton_square():
                dve.wait_ge(newton, 1)
                dve.tensor_tensor(dm_t[:], dm_r[:], dm_r[:], ALU.mult).then_inc(newton, 1)

            def newton_product():
                dve.wait_ge(newton, 2)
                dve.tensor_tensor(dm_q[:], dm_t[:], dm_q[:], ALU.mult).then_inc(newton, 1)

            def newton_factor():
                dve.wait_ge(newton, 3)
                dve.tensor_scalar(dm_t[:], dm_q[:], -0.5, 1.5, ALU.mult, ALU.add).then_inc(newton, 1)

            def newton_result():
                dve.wait_ge(newton, 4)
                dve.tensor_tensor(demod[:], dm_t[:], dm_r[:], ALU.mult).then_inc(newton, 1)

            def scale_down(t):
                dve.wait_ge(down_ps, t.n + 1)
                wait(dve, pre_ready, t.n)
                for g, scaled in ((1, sum_sc[:]), (0, down_bank(t)[:, 0])):
                    tab = down_tab[:, g, t.n, :].unsqueeze(2).to_broadcast([P, HB, S])
                    last = dve.tensor_tensor(scaled.rearrange("p (b s) -> p b s", s=S),
                                             down_bank(t)[:, g].rearrange("p (b s) -> p b s", s=S), tab, ALU.mult)
                last.then_inc(down_scaled, 1)

            def sum_down(t):
                dve.wait_ge(down_scaled, t.n + 1)
                pre = down_bank(t)[:, 0]
                dve.tensor_tensor(pre, pre, sum_sc[:], ALU.add).then_inc(pre_ready, 1)

            def relu_low(t):
                dve.wait_ge(hi_ready, t.n + 1)
                pre = down_bank(t)[:, 0]
                dve.scalar_tensor_tensor(out=act_hl[H:P, t.parity, 0:HT], in0=pre[0:H], scalar=0.0,
                                         in1=act_hl[0:H, t.parity, 0:HT].bitcast(F32), op0=ALU.max, op1=ALU.subtract)
                dve.scalar_tensor_tensor(out=act_hl[0:H, t.parity, HT:T], in0=pre[H:P], scalar=0.0,
                                         in1=act_hl[H:P, t.parity, HT:T].bitcast(F32), op0=ALU.max,
                                         op1=ALU.subtract).then_inc(lo_ready, 1)

            def scale_up(t):
                dve.wait_ge(up_ps, t.n + 1)
                dve.tensor_tensor(by_batch(ps_up[:]), by_batch(ps_up[:]), per_batch(up_tab[:, 0, :, bass.ds(t.n * TB, TB)]),
                                  ALU.mult).then_inc(up_scaled, 1)

            def add_up(t):
                dve.wait_ge(up_scaled, t.n + 1)
                dve.wait_ge(x_doubled, t.n + 1)
                dve.tensor_tensor(x2[:, t.n], ps_up[:], x2[:, t.n], ALU.add).then_inc(up_added, 1)

            def offset_share(t):
                dve.wait_ge(act_sum_ready, t.n + 1)
                dve.tensor_tensor(chunk_by_batch(ps_sum[:]), chunk_by_batch(ps_sum[:]),
                                  chunk_per_batch(up_tab[:, 1, 1, t.n * TB:(t.n + 1) * TB]),
                                  ALU.mult).then_inc(end_off_scaled, 1)

            def add_share(t):
                dve.wait_ge(up_added, t.n + 1)
                if t.n == LAST:
                    dve.wait_ge(end_off_scaled, 1)
                    off = ps_sum[:]
                else:
                    dve.wait_ge(off_scaled, t.n + 1)
                    off = off_sc[:, 1]
                dve.tensor_tensor(x2[:, t.n, 1], off, x2[:, t.n, 1], ALU.add).then_inc(end_x2_ready, 1)

            def modulate_share(t):
                dve.wait_ge(end_x2_ready, shares(t))
                wait(dve, y_ps[DC - 1], t.n - 1)
                dve.tensor_tensor(chunk_by_batch(xm[:, t.parity, 1]), chunk_by_batch(x2[:, t.n, 1]),
                                  chunk_per_batch(style[:, 1, t.n * TB:(t.n + 1) * TB]),
                                  ALU.mult).then_inc(end_xm_ready, 1)

            def demodulate(t, c):
                dve.wait_ge(y_ps[c], t.n + 1)
                tokens = chunk_by_batch(y_bank(t, c))
                dve.tensor_tensor(tokens, tokens, chunk_per_batch(demod[:, c, bass.ds(t.n * TB, TB)]),
                                  ALU.mult).then_inc(y_scaled[c], 1)

            def cap(t, c, biased):
                dve.wait_ge(y_scaled[c], t.n + 1)
                dve.tensor_scalar(y_bank(t, c), y_bank(t, c), 0.0 if biased else vec_cols[:, DC + c:DC + c + 1], CLAMP,
                                  ALU.add, ALU.min).then_inc(y_capped[c], 1)

            def finish(t, c, done):
                dve.wait_ge(y_capped[c], t.n + 1)
                dve.scalar_tensor_tensor(out=z[:, t.parity, c], in0=y_bank(t, c), scalar=-CLAMP, in1=x2[:, t.n, c],
                                         op0=ALU.max, op1=ALU.add).then_inc(done, 1)

            def clip(t, c):
                dve.wait_ge(y_scaled[c], t.n + 1)
                wait(dve, z_ps, t.n - 1)
                dve.tensor_scalar(z[:, t.parity, c], y_bank(t, c), CLAMP, -CLAMP, ALU.min, ALU.max).then_inc(y_capped[c], 1)

            def last_chunk():
                c = DC - 1
                dve.wait_ge(y_ps[c], TILES)
                halves = [slice(part * HT, (part + 1) * HT) for part in range(2)]
                for part in range(2):
                    tokens = chunk_by_batch(y_bank(at(LAST), c)[:, halves[part]])
                    first = LAST * TB + part * HB
                    dve.tensor_tensor(tokens, tokens, chunk_per_batch(demod[:, c, first:first + HB]),
                                      ALU.mult).then_inc(y_scaled[c], 1)
                for part in range(2):
                    tokens = y_bank(at(LAST), c)[:, halves[part]]
                    dve.wait_ge(y_scaled[c], TILES + part)
                    dve.tensor_scalar(tokens, tokens, vec_cols[:, DC + c:DC + c + 1], CLAMP, ALU.add,
                                      ALU.min).then_inc(y_capped[c], 1)
                for part in range(2):
                    dve.wait_ge(y_capped[c], TILES + part)
                    dve.scalar_tensor_tensor(out=z[:, LAST % 2, c, halves[part]],
                                             in0=y_bank(at(LAST), c)[:, halves[part]], scalar=-CLAMP,
                                             in1=x2[:, LAST, c, halves[part]], op0=ALU.max,
                                             op1=ALU.add).then_inc(last_z_ready[c], 1)

            dve.wait_ge(dtab_sb, 1)
            scale_down(at(0))
            sum_down(at(0))
            tables()
            relu_low(at(0))

            scale_down(at(1))
            sum_down(at(1))
            scale_up(at(0))
            relu_low(at(1))
            add_up(at(0))
            add_eps()

            scale_down(at(2))
            sum_down(at(2))
            reciprocal()
            relu_low(at(2))
            newton_square()
            scale_up(at(1))
            newton_product()
            add_up(at(1))
            newton_factor()

            scale_down(at(3))
            newton_result()
            sum_down(at(3))
            dve.wait_ge(newton, 5)
            demodulate(at(0), 0)
            cap(at(0), 0, biased=False)
            finish(at(0), 0, z_ready[0])
            demodulate(at(0), 1)
            cap(at(0), 1, biased=False)
            finish(at(0), 1, z_ready[1])

            def step(tile):
                scale_up(tile(1))
                add_up(tile(1))
                relu_low(tile(0))
                demodulate(tile(2), 1)
                cap(tile(2), 1, biased=False)
                cap(tile(2), 0, biased=True)
                finish(tile(2), 1, z_ready[1])
                finish(tile(2), 0, z_ready[0])
                scale_down(tile(-1))
                sum_down(tile(-1))
            steady(dve, step)

            scale_up(at(LAST - 1))
            add_up(at(LAST - 1))
            relu_low(at(LAST))
            add_share(at(LAST - 1))
            clip(at(LAST - 2), 0)
            modulate_share(at(LAST - 1))

            scale_up(at(LAST))
            clip(at(LAST - 2), 1)
            offset_share(at(LAST))
            add_up(at(LAST))
            add_share(at(LAST))
            modulate_share(at(LAST))
            clip(at(LAST - 1), 0)
            clip(at(LAST - 1), 1)

            demodulate(at(LAST), 0)
            cap(at(LAST), 0, biased=False)
            finish(at(LAST), 0, last_z_ready[0])
            last_chunk()

        @block.gpsimd
        def _(pool):
            pool.memset(ident[:], 0.0).then_inc(zeroed, 1)
            pool.wait_ge(zeroed, 1)
            pool.affine_select(out=ident[:], in_=ident[:], compare_op=ALU.not_equal, fill=1.0, base=0,
                               pattern=[[-1, P]], channel_multiplier=1).then_inc(ident_ready, 1)
            pool.dma_start(aff_sb[:], affine_w.rearrange("(c p) w -> p c w", p=P)).then_inc(aff_in, 16)
            pool.dma_start(vec_rows[0:DC], affine_b.rearrange("(c p) -> c p", p=P)).then_inc(vec_in, 16)
            pool.dma_start(vec_rows[DC:2 * DC], bias.rearrange("(c p) -> c p", p=P)).then_inc(vec_in, 16)
            pool.dma_start(up_sb[0:H, :], up_project).then_inc(up_in, 16)
            pool.dma_start(up_sb[H:P, :], up_project).then_inc(up_in, 16)

            def share(t):
                return 1 if shared(t) else DC

            def weights():
                pool.wait_ge(up_hi_ready, 1)
                pool.tensor_tensor(up_lo[:], up_sb[:], up_hi[:].bitcast(F32), ALU.subtract).then_inc(up_lo_ready, 1)
                pool.wait_ge(wT_sb, 1)
                pool.tensor_tensor(wT_sq[:], wT[:], wT[:], ALU.mult).then_inc(wsq_ready, 1)
                pool.wait_ge(style_sb, 1)
                pool.tensor_tensor(style_sq[:], style[:], style[:], ALU.mult).then_inc(ssq_ready, 1)
                pool.wait_ge(utab_sb, 1)

            def offset_scale(t):
                pool.wait_ge(act_sum_ready, t.n + 1)
                wait(pool, x2_ready, t.n)
                if isinstance(t.n, int) and t.n == LAST:
                    pool.wait_ge(end_x2_ready, 1)
                    chunks = 1
                else:
                    chunks = DC
                sums = by_batch(act_sum[:].unsqueeze(1).to_broadcast([P, chunks, T]))
                pool.tensor_tensor(by_batch(off_sc[:, 0:chunks]), sums,
                                   per_batch(up_tab[:, 1, 0:chunks, bass.ds(t.n * TB, TB)]),
                                   ALU.mult).then_inc(off_scaled, 1)

            def offset_add(t):
                chunks = share(t)
                pool.wait_ge(off_scaled, t.n + 1)
                pool.wait_ge(up_added, t.n + 1)
                pool.tensor_tensor(x2[:, t.n, 0:chunks], x2[:, t.n, 0:chunks], off_sc[:, 0:chunks],
                                   ALU.add).then_inc(x2_ready, 1)

            def offset(t):
                offset_scale(t)
                offset_add(t)

            def modulate(t):
                pool.wait_ge(x2_ready, t.n + 1)
                wait(pool, y_ps[DC - 1], t.n - 1)
                chunks = share(t)
                pool.tensor_tensor(by_batch(xm[:, t.parity, 0:chunks]), by_batch(x2[:, t.n, 0:chunks]),
                                   per_batch(style[:, 0:chunks, bass.ds(t.n * TB, TB)]), ALU.mult).then_inc(xm_ready, 1)

            weights()
            for n in range(FIRST - 1):
                offset(at(n))
                modulate(at(n))

            def step(tile):
                offset(tile(1))
                modulate(tile(1))
            steady(pool, step)

            def add_x2(t, c):
                pool.wait_ge(y_capped[c], t.n + 1)
                pool.tensor_tensor(z[:, t.parity, c], z[:, t.parity, c], x2[:, t.n, c], ALU.add).then_inc(z_ready[c], 1)

            offset(at(LAST - 1))
            modulate(at(LAST - 1))
            add_x2(at(LAST - 2), 0)
            offset_scale(at(LAST))
            add_x2(at(LAST - 2), 1)
            offset_add(at(LAST))
            modulate(at(LAST))
            for c in range(DC):
                add_x2(at(LAST - 1), c)

        @block.tensor
        def _(pe):
            def transpose_in(t):
                pe.wait_ge(x_loaded[t.parity], 16 * (t.half + t.parity))
                wait(pe, x_doubled, t.n)
                wait(pe, out_ready, t.n - 3)
                for c in range(DC):
                    for j in range(TJ):
                        last = pe.transpose(ps_io[:, c * T + j * P:c * T + (j + 1) * P],
                                            x_nat[:, t.parity, j, c * P:(c + 1) * P], ident[:])
                last.then_inc(xT_ps, 1)

            def transpose_first():
                for half, transposed in enumerate((first_xT_ps, xT_ps)):
                    pe.wait_ge(first_x_loaded[half], 16)
                    for c in range(DC):
                        for j in range(TJ // 2):
                            block = half * T + c * HT + j * P
                            last = pe.transpose(ps_io[:, block:block + P],
                                                x_nat[:, 0, half * TJ // 2 + j, c * P:(c + 1) * P], ident[:])
                    last.then_inc(transposed, 1)
                    if half == 0:
                        pe.wait_ge(cond_in, 16)
                        pe.transpose(ps_sum[:, 0:B], cond_sb[:], ident[0:B, 0:B]).then_inc(condT_ps, 1)

            def down(t):
                if isinstance(t.n, int) and t.n == 0:
                    pe.wait_ge(first_xT_sb, 2)
                else:
                    pe.wait_ge(xT_sb, t.n)
                if isinstance(t.n, int) and t.n == 1:
                    pe.wait_ge(dtab_sb, 1)
                else:
                    before = 1 if isinstance(t.n, int) and t.n == 2 else t.n
                    wait(pe, hi_ready, before)
                    wait(pe, lo_ready, before)
                for g in range(2):
                    for c in range(DC):
                        for half in range(2):
                            last = pe.matmul(down_bank(t)[half * H:(half + 1) * H, g],
                                             dp_sb[:, c] if g == 0 else ones[:],
                                             xT[:, t.parity, c, half * HT:(half + 1) * HT],
                                             start=(c == 0), stop=(c == DC - 1))
                last.then_inc(down_ps, 1)

            def up(t):
                pe.wait_ge(hi_ready, t.n + 1)
                pe.wait_ge(lo_ready, t.n + 1)
                wait(pe, up_added, t.n)
                wait(pe, act_sum_ready, t.n)
                for c in range(DC):
                    pe.matmul(ps_up[:, c], up_hi[:, c * P:(c + 1) * P], act_hl[:, t.parity], start=True, stop=False)
                    pe.matmul(ps_up[:, c], up_lo[:, c * P:(c + 1) * P], act_hl[:, t.parity], start=False, stop=True)
                pe.matmul(ps_sum[:], ones_r[:], act_hl[:, t.parity], start=True, stop=True).then_inc(up_ps, 1)

            def linear(t, o):
                if isinstance(t.n, int) and t.n == LAST - 1:
                    pe.wait_ge(y_capped[o], t.n)
                elif not isinstance(t.n, int) or t.n < LAST:
                    wait(pe, z_ready[o], t.n)
                elif o == 1:
                    pe.wait_ge(end_x2_ready, shares(t))
                for i, c in enumerate(reversed(range(DC)) if shared(t) else range(DC)):
                    if c == 0:
                        pe.wait_ge(xm_ready, t.n + 1)
                    elif shared(t):
                        pe.wait_ge(end_xm_ready, shares(t))
                    last = pe.matmul(y_bank(t, o), wT[:, c, o * P:(o + 1) * P], xm[:, t.parity, c],
                                     start=(i == 0), stop=(i == DC - 1))
                last.then_inc(y_ps[o], 1)

            def transpose_out(t):
                pe.wait_ge(x_doubled, min(t.n + 5, TILES) if isinstance(t.n, int) else t.n + 5)
                pe.wait_ge(out_ready, t.n + 1)
                for c in range(DC):
                    pe.wait_ge(z_ready[c], t.n + 1)
                    for j in range(TJ):
                        last = pe.transpose(ps_io[:, j * D + c * P:j * D + (c + 1) * P],
                                            z[:, t.parity, c, j * P:(j + 1) * P], ident[:])
                last.then_inc(z_ps, 1)

            def transpose_last():
                pe.wait_ge(out_ready, LAST + 1)
                pe.wait_ge(last_z_ready[0], 1)
                for part in range(2):
                    pe.wait_ge(last_z_ready[1], 1 + part)
                    for c in range(DC):
                        for j in range(part * TJ // 2, (part + 1) * TJ // 2):
                            last = pe.transpose(ps_io[:, j * D + c * P:j * D + (c + 1) * P],
                                                z[:, LAST % 2, c, j * P:(j + 1) * P], ident[:])
                    last.then_inc(z_ps, 1)

            def keep_busy(count, bank):
                for _ in range(count):
                    pe.matmul(bank[:, 0:P], ident[:], ident[:], start=True, stop=True)

            pe.wait_ge(ident_ready, 1)
            keep_busy(WARM, ps_y[:, 0])
            transpose_first()
            pe.wait_ge(condT_sb, 1)
            pe.wait_ge(dgb_in, 32)
            for g in range(2):
                for half in range(2):
                    last = pe.matmul(ps_y[half * H:(half + 1) * H, 1, g * B:(g + 1) * B], dgb_sb[:, g], condT[:],
                                     start=True, stop=True)
            last.then_inc(dtab_ps, 1)
            pe.wait_ge(aff_in, 16)
            pe.wait_ge(vec_in, 32)
            for c in range(DC):
                pe.transpose(ps_up[:, 1, c * P:(c + 1) * P], aff_sb[:, c], ident[:])
            pe.transpose(ps_up[:, 1, D:D + 2 * DC], vec_rows[:], ident[0:2 * DC, 0:2 * DC]).then_inc(affT_ps, 1)

            def tables():
                pe.wait_ge(ugb_in, 32)
                for g in range(2):
                    for c in range(DC):
                        last = pe.matmul(ps_up[:, 0, (g * DC + c) * B:(g * DC + c + 1) * B],
                                         ugb_sb[:, g, c * P:(c + 1) * P], condT[:], start=True, stop=True)
                last.then_inc(utab_ps, 1)
                pe.wait_ge(affT_sb, 1)
                for c in range(DC):
                    last = pe.matmul(ps_sum[:, c * B:(c + 1) * B], affT[:, c * P:(c + 1) * P], condT[:],
                                     start=True, stop=True)
                last.then_inc(style_ps, 1)

            def transpose_weight():
                pe.wait_ge(w_in, 16)
                for c in range(DC):
                    for o in range(DC):
                        last = pe.transpose(ps_y[:, 0, c * D + o * P:c * D + (o + 1) * P],
                                            w_sb[:, o, c * P:(c + 1) * P], ident[:])
                last.then_inc(wT_ps, 1)

            def norms():
                pe.wait_ge(wT_sb, 1)
                pe.wait_ge(wsq_ready, 1)
                pe.wait_ge(ssq_ready, 1)
                for o in range(DC):
                    for c in range(DC):
                        last = pe.matmul(ps_y[:, 0, o * B:(o + 1) * B], wT_sq[:, c, o * P:(o + 1) * P],
                                         style_sq[:, c], start=(c == 0), stop=(c == DC - 1))
                last.then_inc(norm_ps, 1)

            pe.wait_ge(dp_in, 16)
            pe.wait_ge(ones_ready, 1)
            down(at(0))
            transpose_weight()
            transpose_in(at(1))
            tables()

            down(at(1))
            pe.wait_ge(up_lo_ready, 1)
            pe.wait_ge(utab_sb, 1)
            pe.wait_ge(style_sb, 1)
            transpose_in(at(2))
            up(at(0))
            down(at(2))
            norms()
            transpose_in(at(3))
            up(at(1))
            down(at(3))
            pe.wait_ge(norm_ready, 1)
            for o in range(DC):
                linear(at(0), o)
            up(at(2))

            def step(tile):
                transpose_in(tile(-1))
                for o in range(DC):
                    linear(tile(2), o)
                transpose_out(tile(3))
                down(tile(-1))
                up(tile(0))
            steady(pe, step)

            for o in range(DC):
                linear(at(LAST - 2), o)
            transpose_out(at(LAST - 3))
            up(at(LAST))
            for o in range(DC):
                linear(at(LAST - 1), o)
            transpose_out(at(LAST - 2))
            for o in range(DC):
                linear(at(LAST), o)
            transpose_out(at(LAST - 1))
            transpose_last()


_INS = ['x', 'cond_512', 'L0_cond_down_project', 'L0_cond_down_gamma', 'L0_cond_down_beta', 'L0_cond_up_project',
        'L0_cond_up_gamma', 'L0_cond_up_beta', 'L1_cond_weight', 'L1_cond_bias', 'L1_cond_affine_w',
        'L1_cond_affine_b']
_OUTS = [((64, 64, 256), 'float32')]


def kernel(**inputs):
    import numpy as _np
    import concourse.bacc as _bacc
    from concourse import mybir as _mybir
    from concourse.bass_utils import run_bass_kernel_spmd as _run

    nc = _bacc.Bacc("TRN2", target_bir_lowering=False, num_devices=1)
    arrays, args = {}, []
    for name in _INS:
        a = _np.ascontiguousarray(inputs[name])
        arrays[f"in_{name}_dram"] = a
        args.append(nc.dram_tensor(f"in_{name}_dram", a.shape, _mybir.dt.from_np(a.dtype), kind="ExternalInput").ap())
    for i, (shape, dtype) in enumerate(_OUTS):
        dt = _mybir.dt.from_np(_np.dtype(dtype))
        args.append(nc.dram_tensor(f"out_{i}_dram", shape, dt, kind="ExternalOutput").ap())
    bass_cond_resid(nc, *args)
    r = _run(nc, [arrays], core_ids=[0])
    return r.results[0]["out_0_dram"]
```
